# Optimizing a Trainium2 kernel written in Bass

```python
import numpy as np
import jax
import jax.numpy as jnp

def _softmax(x, axis=-1):
    return jax.nn.softmax(x, axis=axis)

def _gelu(x):
    return jax.nn.gelu(x, approximate=True)

def _silu(x):
    return jax.nn.silu(x)

def _sigmoid(x):
    return jax.nn.sigmoid(x)

def _layernorm(x, axis=-1, eps=1e-05):
    m = jnp.mean(x, axis=axis, keepdims=True)
    v = jnp.var(x, axis=axis, keepdims=True)
    return (x - m) / jnp.sqrt(v + eps)

def _scatter_add(tgt, idx, src, axis=0):
    return tgt.at[idx].add(src)

def _segment_sum(src, seg, n):
    return jax.ops.segment_sum(src, seg, n)
kernel_name = 'mk_lm_tower_d1_tok_ids1024_r4_5ae3b3'

def setup_inputs(seed: int=0):
    np.random.seed(seed)
    _w = jnp.asarray

    def _rec_inputs():
        import jax
        import jax.numpy as jnp
        _rk = jax.random.key(seed)
        x = jax.random.randint(jax.random.fold_in(_rk, 1), (2, 2048), 0, 24991, jnp.int32)
        return x
    x = _rec_inputs()

    def _L0_tok_setup():
        import jax, jax.numpy as jnp
        import numpy as np
        V, R, D = (25000, 64, 256)
        B, S = (8, 512)
        key = jax.random.key(seed)
        k1, k2, k3, k4 = jax.random.split(key, 4)
        input_ids = jax.random.randint(k1, (B, S), 0, V, dtype=jnp.int64 if jax.config.jax_enable_x64 else jnp.int32)
        U = jax.random.normal(k2, (V, R), dtype=jnp.float32)
        s = jax.random.uniform(k3, (R,), dtype=jnp.float32)
        Vt = jax.random.normal(k4, (R, D), dtype=jnp.float32)
        return {'input': input_ids, 'U': U, 's': s, 'Vt': Vt}
    _L0_tok_all = _L0_tok_setup()
    _L0_tok_in = {k: v for k, v in _L0_tok_all.items() if k in ('U', 's', 'Vt')}
    del _L0_tok_all

    def _L0_attn_setup():
        import jax, jax.numpy as jnp
        import numpy as np
        B, S, H, NH = (1, 1024, 256, 16)
        DH = H // NH

        def _split_heads(x):
            b, s, h = x.shape
            return jnp.transpose(x.reshape(b, s, NH, DH), (0, 2, 1, 3))
        key = jax.random.key(seed)
        ks = jax.random.split(key, 9)
        sc = 0.02
        return {'queries': jax.random.normal(ks[0], (B, S, H), jnp.float32), 'keys': jax.random.normal(ks[1], (B, S, H), jnp.float32), 'values': jax.random.normal(ks[2], (B, S, H), jnp.float32), 'Wq_w': jax.random.normal(ks[3], (H, H), jnp.float32) * sc, 'Wq_b': jax.random.normal(ks[4], (H,), jnp.float32) * sc, 'Wk_w': jax.random.normal(ks[5], (H, H), jnp.float32) * sc, 'Wk_b': jax.random.normal(ks[6], (H,), jnp.float32) * sc, 'Wv_w': jax.random.normal(ks[7], (H, H), jnp.float32) * sc, 'Wv_b': jax.random.normal(ks[8], (H,), jnp.float32) * sc}
    _L0_attn_all = _L0_attn_setup()
    _L0_attn_in = {k: v for k, v in _L0_attn_all.items() if k in ('keys', 'values', 'Wq_w', 'Wq_b', 'Wk_w', 'Wk_b', 'Wv_w', 'Wv_b')}
    del _L0_attn_all

    def _L0_ffn_setup():
        import jax, jax.numpy as jnp
        import numpy as np
        H = 256
        E = 8
        B, S = (4, 512)
        key = jax.random.key(seed)
        k1, k2, k3, k4 = jax.random.split(key, 4)
        x = jax.random.normal(k1, (B, S, H), dtype=jnp.float32)
        wg = jax.random.normal(k2, (H, E), dtype=jnp.float32) * 0.02
        W = jax.random.normal(k3, (E, H, H), dtype=jnp.float32) * 0.02
        b = jax.random.normal(k4, (E, H), dtype=jnp.float32) * 0.02
        return {'x': x, 'wg': wg, 'W': W, 'b': b}
    _L0_ffn_all = _L0_ffn_setup()
    _L0_ffn_in = {k: v for k, v in _L0_ffn_all.items() if k in ('wg', 'W', 'b')}
    del _L0_ffn_all
    return {'x': x, 'L0_tok_U': _L0_tok_in['U'], 'L0_tok_s': _L0_tok_in['s'], 'L0_tok_Vt': _L0_tok_in['Vt'], 'L0_attn_keys': _L0_attn_in['keys'], 'L0_attn_values': _L0_attn_in['values'], 'L0_attn_Wq_w': _L0_attn_in['Wq_w'], 'L0_attn_Wq_b': _L0_attn_in['Wq_b'], 'L0_attn_Wk_w': _L0_attn_in['Wk_w'], 'L0_attn_Wk_b': _L0_attn_in['Wk_b'], 'L0_attn_Wv_w': _L0_attn_in['Wv_w'], 'L0_attn_Wv_b': _L0_attn_in['Wv_b'], 'L0_ffn_wg': _L0_ffn_in['wg'], 'L0_ffn_W': _L0_ffn_in['W'], 'L0_ffn_b': _L0_ffn_in['b']}

def reference(x, L0_tok_U, L0_tok_s, L0_tok_Vt, L0_attn_keys, L0_attn_values, L0_attn_Wq_w, L0_attn_Wq_b, L0_attn_Wk_w, L0_attn_Wk_b, L0_attn_Wv_w, L0_attn_Wv_b, L0_ffn_wg, L0_ffn_W, L0_ffn_b):
    import jax
    import jax.numpy as jnp

    def _L0_tok_ref(input, U, s, Vt):
        import jax, jax.numpy as jnp
        import numpy as np
        V, R, D = (25000, 64, 256)
        B, S = (8, 512)
        weight = U * s @ Vt
        return weight[input]

    def _L0_attn_ref(queries, keys, values, Wq_w, Wq_b, Wk_w, Wk_b, Wv_w, Wv_b):
        import jax, jax.numpy as jnp
        import numpy as np
        B, S, H, NH = (1, 1024, 256, 16)
        DH = H // NH

        def _split_heads(x):
            b, s, h = x.shape
            return jnp.transpose(x.reshape(b, s, NH, DH), (0, 2, 1, 3))
        q = jax.nn.relu(queries @ Wq_w.T + Wq_b)
        k = jax.nn.relu(keys @ Wk_w.T + Wk_b)
        v = jax.nn.relu(values @ Wv_w.T + Wv_b)
        qh, kh, vh = (_split_heads(q), _split_heads(k), _split_heads(v))
        score = jnp.einsum('bhsd,bhtd->bhst', qh, kh) / jnp.sqrt(jnp.float32(DH))
        attn = jax.nn.softmax(score, axis=-1)
        a = jnp.einsum('bhst,bhtd->bhsd', attn, vh)
        a = jnp.transpose(a, (0, 1, 3, 2)).reshape(q.shape[0], q.shape[1], q.shape[2])
        return a + queries

    def _L0_ffn_ref(x, wg, W, b):
        import jax, jax.numpy as jnp
        import numpy as np
        H = 256
        E = 8
        B, S = (4, 512)
        Bb, Ss, Hh = x.shape
        Ee = wg.shape[1]
        T = Bb * Ss
        C = T // Ee
        xt = x.reshape(T, Hh)
        logits = xt @ wg
        probs = jax.nn.softmax(logits, axis=-1)
        idx = jnp.argmax(probs, axis=-1)
        mask = jax.nn.one_hot(idx, Ee, dtype=xt.dtype)
        locations = jnp.cumsum(mask, axis=0) - mask
        mask = mask * (locations < C).astype(xt.dtype)
        gate = jnp.sum(probs * mask, axis=-1)
        loc_s = jnp.sum(locations * mask, axis=-1).astype(jnp.int32)
        loc_oh = jax.nn.one_hot(loc_s, C, dtype=xt.dtype)
        dispatch = mask[:, :, None] * loc_oh[:, None, :]
        combine = gate[:, None, None] * dispatch
        exp_in = jnp.einsum('tec,th->ech', dispatch, xt)
        exp_out = jnp.einsum('ech,efh->ecf', exp_in, W) + b[:, None, :]
        out = jnp.einsum('tec,ecf->tf', combine, exp_out)
        return out.reshape(Bb, Ss, Hh)
    h = _L0_tok_ref(x, L0_tok_U, L0_tok_s, L0_tok_Vt)
    h = h + _L0_attn_ref(_layernorm(h, axis=-1), L0_attn_keys, L0_attn_values, L0_attn_Wq_w, L0_attn_Wq_b, L0_attn_Wk_w, L0_attn_Wk_b, L0_attn_Wv_w, L0_attn_Wv_b)
    h = h + _L0_ffn_ref(_layernorm(h, axis=-1), L0_ffn_wg, L0_ffn_W, L0_ffn_b)
    return h

_drawn_inputs = setup_inputs


def setup_inputs(seed=0):
    import zlib

    import numpy as np

    out = dict(_drawn_inputs(seed))
    spreads = {}
    factors = {'L0_attn_keys': 8.0,
     'L0_attn_values': 8.0,
     'L0_attn_Wq_w': 8.0,
     'L0_attn_Wq_b': 8.0,
     'L0_attn_Wk_w': 8.0,
     'L0_attn_Wk_b': 31.036,
     'L0_attn_Wv_w': 8.0,
     'L0_attn_Wv_b': 58.866,
     'L0_ffn_wg': 5.753,
     'L0_ffn_W': 5.506,
     'L0_ffn_b': 64.0}
    for name, (base, spread) in spreads.items():
        noise = np.random.default_rng([zlib.crc32(name.encode()), seed]).standard_normal(out[name].shape)
        drawn = base * np.exp(spread * noise) if base else spread * noise
        out[name] = jnp.asarray(drawn.astype(out[name].dtype))
    for name, factor in factors.items():
        out[name] = (out[name] * factor).astype(out[name].dtype)
    return out
```

```python
from contextlib import ExitStack

import concourse.bass as bass
from concourse import mybir
from concourse.bass import ds

ALU = mybir.AluOpType
ACT = mybir.ActivationFunctionType
AX = mybir.AxisListType
F32 = mybir.dt.float32
BF16 = mybir.dt.bfloat16
I32 = mybir.dt.int32

P = 128
V, R = 25000, 64
H = 256
KC = H // P
B, S, T = 2, 2048, 1024
NH = 16
DH = H // NH
HG = 4
NG = NH // HG
SB = 512
NSB = S // SB
NBLK = B * NG * NSB
TT = T // P
J = 8
TG = P * J
NTG = B * S // TG
E = 8
CAP = B * S // E
EPS = 1e-5
SCALE = float(DH) ** -0.5
PIECES = (0, 0, 0, 1, 1, 2)
KPIECES = (0, 1, 2, 0, 1, 0)
KR = 16 * len(PIECES)
AHEAD = 13
LAST = NBLK * TT
RING = 4


class Chain:

    def __init__(self, eng, sem):
        self.eng, self.sem, self.n = eng, sem, 0

    def mark(self, ins):
        ins.then_inc(self.sem, 1)
        self.n += 1
        return self.n

    def link(self, ins):
        self.mark(ins)
        self.eng.wait_ge(self.sem, self.n)


def build(nc, x, U, s_rank, Vt, keys, values, Wq_w, Wq_b, Wk_w, Wk_b, Wv_w, Wv_b, wg, We, be, out):
    with ExitStack() as ctx:
        def sb(name, shape, dt=F32):
            return ctx.enter_context(nc.sbuf_tensor(name, shape, dt))

        def sem(name):
            return ctx.enter_context(nc.semaphore(name))

        q_dram = nc.dram_tensor("q_dram", (3, NBLK, HG * DH, SB), BF16).ap()
        k_dram = nc.dram_tensor("k_dram", (3, H, T), BF16).ap()
        a_dram = nc.dram_tensor("a_dram", (NBLK, P, SB), F32).ap()
        xd_dram = nc.dram_tensor("xd_dram", (2 * E * CAP, H), F32).ap()
        yd_dram = nc.dram_tensor("yd_dram", (E * CAP, H), F32).ap()

        res = sb("res", [P, NTG, J * H])
        kst = sb("kst", [P, NH * T], BF16)
        qst = sb("qst", [P, 4, HG, SB], BF16)
        vaug = sb("vaug", [P, NG, TT * HG * 32])
        vblk = sb("vblk", [P, TT, HG, 32])
        probs = sb("probs", [P, 2 * RING, 2 * SB])
        acc = sb("acc", [P, 2, SB])
        ident = sb("ident", [P, P])
        identb = sb("identb", [P, P], BF16)
        upper = sb("upper", [P, P])
        ones = sb("ones", [P, P])
        mx = sb("mx", [P, 2, 2, 16])
        mxb = sb("mxb", [P, 16])
        mpc = sb("mpc", [P, 32], BF16)
        mrow = sb("mrow", [P, 32], BF16)
        idx = sb("idx", [P, NTG * J], I32)
        idxg = sb("idxg", [P, J], I32)
        srank = sb("srank", [R, 1])
        vt = sb("vt", [R, H])
        bq = sb("bq", [P, KC])
        bk = sb("bk", [P, KC])
        bv = sb("bv", [1, H])
        bexp = sb("bexp", [1, E * H])
        wgs = sb("wgs", [P, KC, E])
        gemb = sb("gemb", [P, J, R])
        uT = sb("uT", [R, J * P])
        wload = sb("wload", [P, 3, KC, H])
        wT = sb("wT", [P, 3, KC, H])
        pieces = sb("pieces", [P, 3, KC, T], BF16)
        stats = sb("stats", [P, J, 6])
        mv = sb("mv", [P, J, 2])
        std = sb("std", [P, J])
        rstd = sb("rstd", [P, J])
        eidi = sb("eidi", [P, E], I32)
        eid = sb("eid", [P, E])
        rank8 = sb("rank8", [P, E])
        tidi = sb("tidi", [P, J], I32)
        tid = sb("tid", [P, J])
        lg = sb("lg", [P, J, E])
        ex = sb("ex", [P, J, E])
        oh = sb("oh", [P, J, E])
        loc = sb("loc", [P, J, E])
        tmp = sb("tmp", [P, J, E])
        c1 = sb("c1", [P, J])
        c2 = sb("c2", [P, J])
        c3 = sb("c3", [P, J])
        slot = sb("slot", [P, J])
        kept = sb("kept", [P, J])
        cnt = sb("cnt", [P, E])
        base = sb("base", [P, E])
        run = sb("run", [P, E])
        sidx = sb("sidx", [P, J], I32)
        gates = sb("gates", [P, NTG, J])
        gidx = sb("gidx", [P, NTG * J], I32)
        gidxg = sb("gidxg", [P, J], I32)
        gateg = sb("gateg", [P, J])

        def view(k):
            return probs[:, 2 * k:2 * k + 2, :].rearrange("p a b -> p (a b)")
        y_v = view(0).rearrange("p (j h) -> p j h", j=J)
        yT_v = view(1).rearrange("p (k t) -> p k t", k=KC)
        q32_v = view(2).rearrange("p (k t) -> p k t", k=KC)
        r_v = view(3).rearrange("p (k t) -> p k t", k=KC)
        kv_load = y_v
        qst32 = qst[:, :, :, :].rearrange("p a b c -> p (a b c)").bitcast(F32)
        kst32 = kst[:, :].bitcast(F32)
        y2_v = q32_v.rearrange("p k t -> p (k t)").rearrange("p (j h) -> p j h", j=J)
        y2T_v = r_v
        eps_t = sb("eps_t", [P, 1])
        TC, TA, TB = 55, 20, 34
        We_load = kst32[:, 0:512].rearrange("p (c h) -> p c h", c=KC)
        We_T = kst32[:, 512:1024].rearrange("p (c h) -> p c h", c=KC)
        x_load = kst32[:, 1024:2048].rearrange("p (n h) -> p n h", n=4)
        xe_T = kst32[:, 2048:3072].rearrange("p (c t) -> p c t", c=KC)
        y_out = kst32[:, 3072:4096].rearrange("p (n h) -> p n h", n=4)
        got = kst32[:, 4096:6144].rearrange("p (j h) -> p j h", j=J)


        ps = ctx.enter_context(nc.psum_tensor("ps", [P, 8, 512], F32))
        MAX_BANK, PV_BANK = 3, 7
        EXP_BANK = (0, 1, 2, 1)
        EXP_BACK = (4, 2, 4, 2)

        names = """w_loaded c_loaded kv_loaded idx_loaded const_made wT_ready wT_kept kvT_ready kvT_kept
            proj_ready proj_kept kv_sum pieces_ready pieces_stored k_stacked ones_set
            idx_picked rows_gathered uT_ready uT_kept emb_ready y_ready yT_ready yT_kept q_ready q_kept
            std_ready q_pieces_ready q_pieces_stored prelude_chain
            q_loaded va_loaded vb_loaded scores_ready exp_done pv_done max_ready max_done max_chain
            mpc_ready mrow_ready m_loaded acc_ready acc_stored
            zeroed att_loaded t_chain tT_ready tT_kept lg_ready ex_ready t_std cnt_ready pre_ready
            sidx_ready scattered eload eT_ready eT_kept e_ready e_kept e_stored gidx_picked gathered
            final_ready out_stored f_chain zset p_chain ohs sp_go pool_go pe_go dve_go""".split()
        sm = {n: sem(n) for n in names}

        def stand(eng, name):
            eng.sem_inc(sm[name], 1)

        block = ctx.enter_context(nc.Block())

        @block.sync
        def _(sp):
            for n, w in enumerate((Wq_w, Wk_w, Wv_w)):
                sp.dma_start(wload[:, n], w.rearrange("(c p) h -> p c h", p=P)).then_inc(sm["w_loaded"], 16)
            sp.dma_start(idx[:, :].rearrange("p (b h j) -> p b h j", b=B, j=J),
                         x.rearrange("b (h p j) -> p b h j", p=P, j=J)).then_inc(sm["idx_loaded"], 16)
            sp.dma_start(kv_load, keys.rearrange("o (n p) h -> p (o n) h", p=P)).then_inc(sm["kv_loaded"], 16)
            sp.dma_start(bq[:, :], Wq_b.rearrange("(c p) -> p c", p=P), allow_slow_non_contiguous=True).then_inc(sm["c_loaded"], 16)
            sp.dma_start(bk[:, :], Wk_b.rearrange("(c p) -> p c", p=P), allow_slow_non_contiguous=True).then_inc(sm["c_loaded"], 16)
            sp.dma_start(bv[:, :], Wv_b.rearrange("(o h) -> o h", o=1)).then_inc(sm["c_loaded"], 16)
            sp.dma_start(bexp[:, :], be.rearrange("(o e) h -> o (e h)", o=1)).then_inc(sm["c_loaded"], 16)
            sp.dma_start(srank[:, :], s_rank.rearrange("(r o) -> r o", o=1), allow_slow_non_contiguous=True).then_inc(sm["c_loaded"], 16)
            sp.dma_start(vt[:, :], Vt).then_inc(sm["c_loaded"], 16)
            sp.dma_start(wgs[:, :, :], wg.rearrange("(c p) e -> p c e", p=P)).then_inc(sm["c_loaded"], 16)
            sp.wait_ge(sm["zset"], 1)
            for n in range(4):
                sp.dma_start(xd_dram[n * TG:(n + 1) * TG, :].rearrange("(p j) h -> p (j h)", p=P),
                             kst32[:, 0:2048]).then_inc(sm["zeroed"], 16)
            sp.wait_ge(sm["pieces_ready"], 1)
            for r in range(3):
                sp.dma_start(k_dram[r].rearrange("(c p) t -> p c t", p=P), pieces[:, r]).then_inc(sm["pieces_stored"], 16)
            sp.wait_ge(sm["kvT_ready"], 4)
            sp.dma_start(kv_load, values.rearrange("o (n p) h -> p (o n) h", p=P)).then_inc(sm["kv_loaded"], 16)
            sp.wait_ge(sm["pieces_stored"], 48)
            sp.wait_ge(sm["zeroed"], 64)
            for r, pc in enumerate(KPIECES):
                sp.dma_start(kst[16 * r:16 * r + 16, :].rearrange("p (h t) -> p h t", h=NH),
                             k_dram[pc].rearrange("(h i) t -> i h t", i=DH)).then_inc(sm["k_stacked"], 16)
            with sp.Fori(0, NTG) as g:
                sp.wait_ge(sm["q_pieces_ready"], g + 1)
                stand(sp, "sp_go")
                for r in range(3):
                    for c in range(KC):
                        for hh in range(2):
                            dst = q_dram[r, ds((g // 2) * 16 + (g % 2) * 2 + (2 * c + hh) * 4, 2)]
                            sp.dma_start(dst.rearrange("n p s -> p n s"),
                                         pieces[64 * hh:64 * hh + 64, r, c].rearrange("p (n s) -> p n s", n=2)
                                         ).then_inc(sm["q_pieces_stored"], 16)
            sp.wait_ge(sm["q_pieces_stored"], NTG * 12 * 16)

            def load_q(i):
                for r, pc in enumerate(PIECES):
                    sp.dma_start(qst[16 * r:16 * r + 16, ds(i % 4, 1)].rearrange("p o j s -> p (o j) s"),
                                 q_dram[pc, ds(i, 1)].rearrange("o (j i) s -> (o i) j s", i=DH)
                                 ).then_inc(sm["q_loaded"], 16)

            def load_v(i, half):
                n = HALF_V
                sp.dma_start(vblk[:, 4 * half:4 * half + 4].rearrange("p t j c -> p (t j c)"),
                             vaug[:, ds((i // NSB) % NG, 1), half * n:(half + 1) * n].rearrange("p o n -> p (o n)")
                             ).then_inc(sm["vb_loaded" if half else "va_loaded"], 16)

            def load_m(i):
                sp.wait_ge(sm["mrow_ready"], i + 1)
                for c in range(2):
                    row = qst[KR + c:KR + c + 1, ds(i % 4, 1)].rearrange("p o j (t q s) -> p (o j t) q s", q=4, s=32)
                    for q in range(4):
                        sp.dma_start(row[:, :, q, :], mrow[32 * q + 16 * c:32 * q + 16 * c + 16, :]
                                     ).then_inc(sm["m_loaded"], 16)

            HALF_V = 4 * HG * 32
            sp.wait_ge(sm["ones_set"], 2)
            sp.wait_ge(sm["proj_kept"], 8)
            for i in range(3):
                load_q(i)
                if i < 2:
                    sp.wait_ge(sm["q_loaded"], 96 * (i + 1))
            load_v(0, 0)
            load_m(0)

            def store_acc(i):
                sp.wait_ge(sm["acc_ready"], i + 1)
                sp.dma_start(a_dram[ds(i, 1)].rearrange("o p s -> (o p) s"),
                             acc[:, ds(i % 2, 1)].rearrange("p o s -> p (o s)")).then_inc(sm["acc_stored"], 16)

            def block_sp(i, first=False, more_q=True, more=True):
                sp.wait_ge(sm["pv_done"], TT * i)
                load_v(i, 1)
                if not first:
                    store_acc(i - 1)
                if more_q:
                    sp.wait_ge(sm["scores_ready"], HG * TT * i)
                    sp.wait_ge(sm["q_loaded"], 96 * (i + 3))
                    load_q(i + 3)
                if more:
                    load_m(i + 1)
                    sp.wait_ge(sm["pv_done"], TT * i + 4)
                    load_v(i + 1, 0)

            block_sp(0, first=True)
            with sp.Fori(1, NBLK - 3) as i:
                block_sp(i)
            for i in range(NBLK - 3, NBLK):
                block_sp(i, more_q=False, more=i < NBLK - 1)
            store_acc(NBLK - 1)
            sp.wait_ge(sm["acc_stored"], 16 * NBLK)

            with sp.Fori(0, NTG) as g:
                sp.wait_ge(sm["tT_ready"], 4 * g)
                stand(sp, "sp_go")
                for q in range(2):
                    for part, dst in ((0, y_v), (DH, yT_v)):
                        for j in range(HG):
                            src = a_dram[ds(8 * g + 4 * q, 4), 32 * j + part:32 * j + part + DH]
                            p0 = 64 * q + DH * j
                            d = dst[p0:p0 + DH].rearrange("p a b -> p (a b)").rearrange("p (n s) -> p n s", n=4)
                            sp.dma_start(d, src.rearrange("n x s -> x n s")).then_inc(sm["att_loaded"], 16)

            with sp.Fori(0, E) as e:
                sp.wait_ge(sm["scattered"], NTG * J * 16)
                sp.wait_ge(sm["eT_ready"], 3 * e)
                stand(sp, "sp_go")
                sp.dma_start(We_load, We[ds(e, 1)].rearrange("o (c p) h -> p (o c) h", p=P)).then_inc(sm["eload"], 16)
                sp.dma_start(x_load, xd_dram[ds(e * CAP, CAP)].rearrange("(n p) h -> p n h", p=P)).then_inc(sm["eload"], 16)
                sp.wait_ge(sm["e_kept"], 2 * e + 2)
                sp.dma_start(yd_dram[ds(e * CAP, CAP)].rearrange("(n p) h -> p n h", p=P), y_out).then_inc(sm["e_stored"], 16)
            with sp.Fori(0, NTG) as g:
                sp.wait_ge(sm["final_ready"], g + 1)
                stand(sp, "sp_go")
                sp.dma_start(out[ds(g * TG, TG)].rearrange("(p j) h -> p (j h)", p=P),
                             res[:, ds(g, 1)].rearrange("p o n -> p (o n)")).then_inc(sm["out_stored"], 16)
            sp.wait_ge(sm["out_stored"], 16 * NTG)

        @block.gpsimd
        def _(pool):
            ch = Chain(pool, sm["p_chain"])
            ch.link(pool.memset(ident[:, :], 0.0))
            ch.link(pool.memset(upper[:, :], 1.0))
            ch.link(pool.affine_select(out=ident[:, :], in_=ident[:, :], compare_op=ALU.not_equal, fill=1.0,
                                       base=0, pattern=[[-1, P]], channel_multiplier=1))
            ch.link(pool.affine_select(out=upper[:, :], in_=upper[:, :], compare_op=ALU.is_gt, fill=0.0,
                                       base=0, pattern=[[1, P]], channel_multiplier=-1))
            ch.link(pool.iota(eidi[:, :], [[1, E]], 0, 0))
            ch.link(pool.iota(tidi[:, :], [[1, J]], E * CAP, J))
            ch.link(pool.tensor_copy(identb[:, :], ident[:, :]))
            ch.link(pool.tensor_copy(eid[:, :], eidi[:, :]))
            ch.link(pool.tensor_copy(tid[:, :], tidi[:, :]))
            pool.tensor_scalar(rank8[:, :], eid[:, :], -1.0, float(E), ALU.mult, ALU.add).then_inc(sm["const_made"], 1)
            pool.wait_ge(sm["idx_loaded"], 16)
            with pool.Fori(0, NTG) as g:
                pool.wait_ge(sm["rows_gathered"], 16 * J * g)
                pool.tensor_copy(idxg[:, :], idx[:, ds(g * J, J)]).then_inc(sm["idx_picked"], 1)
                pool.wait_ge(sm["idx_picked"], g + 1)
                pool.wait_ge(sm["uT_ready"], 2 * g)
                stand(pool, "pool_go")
                for j in range(J):
                    pool.indirect_dma_start(gemb[:, j], None, U, bass.IndirectOffsetOnAxis(ap=idxg[:, j:j + 1], axis=0)
                                            ).then_inc(sm["rows_gathered"], 16)
            with pool.Fori(0, NTG) as g:
                pool.wait_ge(sm["sidx_ready"], g + 1)
                stand(pool, "pool_go")
                for j in range(J):
                    pool.indirect_dma_start(xd_dram, bass.IndirectOffsetOnAxis(ap=sidx[:, j:j + 1], axis=0), y2_v[:, j], None
                                            ).then_inc(sm["scattered"], 16)
            pool.wait_ge(sm["e_stored"], 16 * E)
            with pool.Fori(0, NTG) as g:
                pool.wait_ge(sm["gathered"], 16 * J * g)
                pool.wait_ge(sm["final_ready"], g)
                pool.tensor_copy(gidxg[:, :], gidx[:, ds(g * J, J)]).then_inc(sm["gidx_picked"], 1)
                pool.wait_ge(sm["gidx_picked"], g + 1)
                stand(pool, "pool_go")
                for j in range(J):
                    pool.indirect_dma_start(got[:, j], None, yd_dram, bass.IndirectOffsetOnAxis(ap=gidxg[:, j:j + 1], axis=0)
                                            ).then_inc(sm["gathered"], 16)


        @block.tensor
        def _(pe):
            pe.wait_ge(sm["w_loaded"], 48)
            pe.wait_ge(sm["const_made"], 1)
            for w in range(3):
                for k in range(KC):
                    for c in range(KC):
                        mm = pe.transpose(ps[:, w, (k * KC + c) * P:(k * KC + c + 1) * P],
                                          wload[:, w, c, k * P:(k + 1) * P], ident[:, :])
                mm.then_inc(sm["wT_ready"], 1)

            def turn_kv(bank, first):
                for k in range(KC):
                    for q in range(2):
                        if not first:
                            pe.wait_ge(sm["kvT_kept"], 4)
                        for n in range(4):
                            mm = pe.transpose(ps[:, bank + 2 * k + q, n * P:(n + 1) * P],
                                              kv_load[:, 4 * q + n, k * P:(k + 1) * P], ident[:, :])
                        mm.then_inc(sm["kvT_ready"], 1)

            pe.wait_ge(sm["kv_loaded"], 16)
            turn_kv(3, True)
            pe.wait_ge(sm["wT_kept"], 3)
            pe.wait_ge(sm["kvT_kept"], 4)
            for c in range(KC):
                for n in range(2):
                    for k in range(KC):
                        mm = pe.matmul(ps[:, 3 + 2 * c + n, :], wT[:, 1, k, c * P:(c + 1) * P],
                                       yT_v[:, k, n * 512:(n + 1) * 512], start=(k == 0), stop=(k == 1))
                    mm.then_inc(sm["proj_ready"], 1)
            pe.wait_ge(sm["kv_loaded"], 32)
            pe.wait_ge(sm["proj_kept"], 4)
            turn_kv(3, False)
            pe.wait_ge(sm["kvT_kept"], 8)
            pe.wait_ge(sm["c_loaded"], 7 * 16)
            pe.wait_ge(sm["ohs"], 1)
            for n in range(TT):
                o = ps[:, 3 + n // 2, (n % 2) * H:(n % 2 + 1) * H]
                for k in range(KC):
                    pe.matmul(o, yT_v[:, k, n * P:(n + 1) * P], wT[:, 2, k, :], start=(k == 0), stop=False)
                mm = pe.matmul(o, ones[0:1, :], bv[:, :], start=False, stop=True)
                if n % 2:
                    mm.then_inc(sm["proj_ready"], 1)
            pe.wait_ge(sm["proj_kept"], 8)
            with pe.Fori(0, NTG) as g:
                pe.wait_ge(sm["rows_gathered"], 16 * J * (g + 1))
                pe.wait_ge(sm["yT_kept"], 4 * g)
                stand(pe, "pe_go")
                for q in range(2):
                    for n in range(4):
                        mm = pe.transpose(ps[0:R, q, n * P:(n + 1) * P], gemb[:, 4 * q + n, :], ident[:, :])
                    mm.then_inc(sm["uT_ready"], 1)
                pe.wait_ge(sm["uT_kept"], 2 * g + 2)
                pe.wait_ge(sm["q_kept"], 4 * g)
                for j in range(J):
                    mm = pe.matmul(ps[:, 2 + j // 2, (j % 2) * H:(j % 2 + 1) * H], uT[:, j * P:(j + 1) * P], vt[:, :],
                                   start=True, stop=True)
                mm.then_inc(sm["emb_ready"], 1)
                pe.wait_ge(sm["y_ready"], g + 1)
                for k in range(KC):
                    for q in range(2):
                        for n in range(4):
                            mm = pe.transpose(ps[:, (6 + 2 * k + q) % 8, n * P:(n + 1) * P],
                                              y_v[:, 4 * q + n, k * P:(k + 1) * P], ident[:, :])
                        mm.then_inc(sm["yT_ready"], 1)
                pe.wait_ge(sm["yT_kept"], 4 * g + 4)
                for c in range(KC):
                    for n in range(2):
                        for k in range(KC):
                            mm = pe.matmul(ps[:, 2 + 2 * c + n, :], wT[:, 0, k, c * P:(c + 1) * P],
                                           yT_v[:, k, n * 512:(n + 1) * 512], start=(k == 0), stop=(k == 1))
                        mm.then_inc(sm["q_ready"], 1)

            pe.wait_ge(sm["k_stacked"], 6 * 16)
            pe.wait_ge(sm["ones_set"], 2)
            pe.wait_ge(sm["q_kept"], 4 * NTG)
            pe.wait_ge(sm["const_made"], 1)

            def maximum(m, t, gi, u):
                if t == 0 and u == 0:
                    pe.wait_ge(sm["q_loaded"], 96 * (m + 1))
                hg = (m // NSB) % NG
                j, half, st = 2 * (t % 2) + u // 2, u % 2, t // 2
                if not (isinstance(gi, int) and gi == 0):
                    pe.wait_ge(sm["max_done"], 4 * gi + u - 3)
                pe.matmul(ps[:, MAX_BANK + u, :],
                          qst[0:KR, ds(m % 4, 1), j, st * P:(st + 1) * P].rearrange("p o s -> p (o s)"),
                          kst[0:KR, ds((hg * HG + j) * T + half * 512, 512)],
                          start=True, stop=True).then_inc(sm["max_ready"], 1)

            def score(i, t, j):
                hg = (i // NSB) % NG
                n = HG * TT * i + HG * t + j + 1 - EXP_BACK[j]
                if not (isinstance(n, int) and n < 1):
                    pe.wait_ge(sm["exp_done"], n)
                pe.matmul(ps[:, EXP_BANK[j], :], kst[0:KR + 2, ds((hg * HG + j) * T + t * P, P)],
                          qst[0:KR + 2, ds(i % 4, 1), j, :].rearrange("p o s -> p (o s)"),
                          start=True, stop=True).then_inc(sm["scores_ready"], 1)

            def pv(i, t):
                pe.wait_ge(sm["exp_done"], HG * (TT * i + t + 1))
                if t == 0:
                    pe.wait_ge(sm["va_loaded"], 16 * (i + 1))
                    pe.wait_ge(sm["acc_ready"], i)
                if t == 4:
                    pe.wait_ge(sm["vb_loaded"], 16 * (i + 1))
                for j in range(HG):
                    mm = pe.matmul(ps[32 * j:32 * j + 32, PV_BANK, :], vblk[:, t, j, :],
                                   probs[:, 2 * (t % RING) + j // 2, (j % 2) * SB:(j % 2 + 1) * SB],
                                   start=(t == 0), stop=(t == TT - 1))
                mm.then_inc(sm["pv_done"], 1)

            def block_pe(i, first=False, ahead=TT):
                pe.wait_ge(sm["m_loaded"], 128 * (i + 1))
                for t in range(TT):
                    far = t + AHEAD
                    for step in "s0 m0 s1 s2 m1 pv s3 m2 m3".split():
                        if step[0] == "s":
                            score(i, t, int(step[1]))
                        elif step == "pv":
                            if t:
                                pv(i, t - 1)
                            elif not first:
                                pv(i - 1, TT - 1)
                        elif t < ahead:
                            maximum(i + far // TT, far % TT, TT * i + far, int(step[1]))

            for gi in range(AHEAD):
                for u in range(4):
                    maximum(gi // TT, gi % TT, gi, u)
            block_pe(0, first=True)
            with pe.Fori(1, NBLK - 2) as i:
                block_pe(i)
            block_pe(NBLK - 2, ahead=2 * TT - AHEAD)
            block_pe(NBLK - 1, ahead=0)
            pv(NBLK - 1, TT - 1)
            pe.wait_ge(sm["acc_ready"], NBLK)
            pe.wait_ge(sm["max_done"], 4 * LAST)

            with pe.Fori(0, NTG) as g:
                pe.wait_ge(sm["t_std"], g + 1)
                pe.wait_ge(sm["tT_kept"], 4 * g)
                for k in range(KC):
                    for q in range(2):
                        for n in range(4):
                            mm = pe.transpose(ps[:, 2 * k + q, n * P:(n + 1) * P],
                                              y2_v[:, 4 * q + n, k * P:(k + 1) * P], ident[:, :])
                        mm.then_inc(sm["tT_ready"], 1)
                pe.wait_ge(sm["tT_kept"], 4 * g + 4)
                for j in range(J):
                    for k in range(KC):
                        mm = pe.matmul(ps[:, 4, j * E:(j + 1) * E], y2T_v[:, k, j * P:(j + 1) * P], wgs[:, k, :],
                                       start=(k == 0), stop=(k == 1))
                mm.then_inc(sm["lg_ready"], 1)
                pe.wait_ge(sm["cnt_ready"], g + 1)
                pe.matmul(ps[:, 5, 0:E], upper[:, :], cnt[:, :], start=True, stop=True)
                pe.matmul(ps[:, 6, 0:E], ones[:, :], cnt[:, :], start=True, stop=True).then_inc(sm["pre_ready"], 1)

            with pe.Fori(0, E) as e:
                pe.wait_ge(sm["eload"], 32 * (e + 1))
                for k in range(KC):
                    for c in range(KC):
                        mm = pe.transpose(ps[:, 0, (k * KC + c) * P:(k * KC + c + 1) * P],
                                          We_load[:, c, k * P:(k + 1) * P], ident[:, :])
                mm.then_inc(sm["eT_ready"], 1)
                for k in range(KC):
                    for n in range(4):
                        mm = pe.transpose(ps[:, 1 + k, n * P:(n + 1) * P], x_load[:, n, k * P:(k + 1) * P], ident[:, :])
                    mm.then_inc(sm["eT_ready"], 1)
                pe.wait_ge(sm["eT_kept"], 3 * e + 3)
                pe.wait_ge(sm["e_kept"], 2 * e)
                for n in range(4):
                    o = ps[:, 3 + n // 2, (n % 2) * H:(n % 2 + 1) * H]
                    for k in range(KC):
                        pe.matmul(o, xe_T[:, k, n * P:(n + 1) * P], We_T[:, k, :], start=(k == 0), stop=False)
                    mm = pe.matmul(o, ones[0:1, :], bexp[:, ds(e * H, H)], start=False, stop=True)
                    if n % 2:
                        mm.then_inc(sm["e_ready"], 1)

        @block.scalar
        def _(act):
            act.wait_ge(sm["c_loaded"], 7 * 16)
            for n in range(4):
                act.wait_ge(sm["proj_ready"], n + 1)
                act.activation(q32_v[:, n // 2, (n % 2) * 512:(n % 2 + 1) * 512], ps[:, 3 + n, :], ACT.Relu,
                               bias=bk[:, n // 2:n // 2 + 1]).then_inc(sm["proj_kept"], 1)
            act.wait_ge(sm["ones_set"], 1)
            for n in range(4):
                act.wait_ge(sm["proj_ready"], 5 + n)
                for u in range(2):
                    tt = 2 * n + u
                    dst = vaug[:, :, :].rearrange("p g (t j c) -> p g t j c", t=TT, j=HG)[:, :, tt, :, 0:DH]
                    ins = act.activation(dst, ps[:, 3 + n, u * H:(u + 1) * H].rearrange("p (g j c) -> p g j c", g=NG, j=HG),
                                         ACT.Relu)
                ins.then_inc(sm["proj_kept"], 1)
            with act.Fori(0, NTG) as g:
                act.wait_ge(sm["prelude_chain"], 36 * g + 16)
                act.activation(std[:, :], mv[:, :, 1], ACT.Sqrt, bias=eps_t[:, 0:1]).then_inc(sm["std_ready"], 1)
                act.wait_ge(sm["q_pieces_ready"], g)
                for n in range(4):
                    act.wait_ge(sm["q_ready"], 4 * g + n + 1)
                    act.activation(q32_v[:, n // 2, (n % 2) * 512:(n % 2 + 1) * 512], ps[:, 2 + n, :], ACT.Relu,
                                   bias=bq[:, n // 2:n // 2 + 1]).then_inc(sm["q_kept"], 1)
            act.wait_ge(sm["q_pieces_ready"], NTG)

            def exps(i, t):
                for j in range(HG):
                    act.wait_ge(sm["scores_ready"], HG * (TT * i + t) + j + 1)
                    if not (isinstance(i, int) and i == 0 and t < RING) and j == 0:
                        act.wait_ge(sm["pv_done"], TT * i + t - RING + 1)
                    act.activation(probs[:, 2 * (t % RING) + j // 2, (j % 2) * SB:(j % 2 + 1) * SB],
                                   ps[:, EXP_BANK[j], :], ACT.Exp, scale=SCALE).then_inc(sm["exp_done"], 1)

            def keep_acc(i):
                act.wait_ge(sm["pv_done"], TT * (i + 1))
                act.wait_ge(sm["acc_stored"], 16 * (i - 1))
                act.activation(acc[:, ds(i % 2, 1)].rearrange("p o s -> p (o s)"), ps[:, PV_BANK, :], ACT.Copy
                               ).then_inc(sm["acc_ready"], 1)

            def block_act(i, first=False):
                for t in range(TT):
                    exps(i, t)
                    if t == 0 and not first:
                        keep_acc(i - 1)

            block_act(0, first=True)
            exps(1, 0)
            act.wait_ge(sm["pv_done"], TT)
            act.activation(acc[:, 0, :], ps[:, PV_BANK, :], ACT.Copy).then_inc(sm["acc_ready"], 1)
            for t in range(1, TT):
                exps(1, t)
            with act.Fori(2, NBLK - 1) as i:
                block_act(i)
            block_act(NBLK - 1)
            keep_acc(NBLK - 1)

            with act.Fori(0, NTG) as g:
                act.wait_ge(sm["t_chain"], TC * g + TA)
                act.activation(std[:, :], mv[:, :, 1], ACT.Sqrt, bias=eps_t[:, 0:1]).then_inc(sm["std_ready"], 1)
                act.wait_ge(sm["t_chain"], TC * g + TB)
                act.activation(ex[:, :, :], lg[:, :, :], ACT.Exp).then_inc(sm["ex_ready"], 1)
            with act.Fori(0, E) as e:
                act.wait_ge(sm["e_stored"], 16 * e)
                for n in range(2):
                    act.wait_ge(sm["e_ready"], 2 * e + n + 1)
                    act.activation(y_out[:, 2 * n:2 * n + 2].rearrange("p a h -> p (a h)"), ps[:, 3 + n, :], ACT.Copy
                                   ).then_inc(sm["e_kept"], 1)


        @block.vector
        def _(dve):
            dve.memset(kst32[:, 0:2048], 0.0).then_inc(sm["zset"], 1)
            dve.memset(vaug[:, :, :], 1.0).then_inc(sm["ones_set"], 1)
            dve.memset(ones[:, :], 1.0).then_inc(sm["ohs"], 1)
            dve.memset(eps_t[:, :], EPS).then_inc(sm["ohs"], 1)
            dve.memset(base[:, :], 0.0).then_inc(sm["ohs"], 1)
            for w in range(3):
                dve.wait_ge(sm["wT_ready"], w + 1)
                dve.tensor_copy(wT[:, w].rearrange("p c h -> p (c h)"), ps[:, w, :]).then_inc(sm["wT_kept"], 1)

            def keep_kv(n0):
                for n in range(4):
                    dve.wait_ge(sm["kvT_ready"], n0 + n + 1)
                    if n0:
                        dve.wait_ge(sm["proj_ready"], 4)
                    dve.tensor_copy(yT_v[:, n // 2, (n % 2) * 512:(n % 2 + 1) * 512], ps[:, 3 + n, :]).then_inc(sm["kvT_kept"], 1)

            def split(ch):
                ch.link(dve.tensor_copy(pieces[:, 0], q32_v))
                ch.link(dve.tensor_tensor(r_v, q32_v, pieces[:, 0], ALU.subtract))
                ch.link(dve.tensor_copy(pieces[:, 1], r_v))
                return dve.tensor_tensor(pieces[:, 2], r_v, pieces[:, 1], ALU.subtract)

            keep_kv(0)
            dve.wait_ge(sm["proj_kept"], 4)
            split(Chain(dve, sm["kv_sum"])).then_inc(sm["pieces_ready"], 1)
            keep_kv(4)
            dve.wait_ge(sm["zeroed"], 64)
            dve.memset(kst[KR:KR + 32, :], 1.0).then_inc(sm["ones_set"], 1)

            dve.wait_ge(sm["pieces_stored"], 48)
            dve.wait_ge(sm["ohs"], 3)
            with dve.Fori(0, NTG) as g:
                b0 = 36 * g
                n = 0
                for q in range(2):
                    dve.wait_ge(sm["uT_ready"], 2 * g + q + 1)
                    dve.tensor_scalar(uT[:, q * 512:(q + 1) * 512], ps[0:R, q, :], srank[:, 0:1], None, ALU.mult
                                      ).then_inc(sm["uT_kept"], 1)
                dve.wait_ge(sm["emb_ready"], g + 1)
                emb = lambda j: ps[:, 2 + j // 2, (j % 2) * H:(j % 2 + 1) * H]
                stand(dve, "dve_go")
                for j in range(J):
                    dve.bn_stats(stats[:, j, :], emb(j)).then_inc(sm["prelude_chain"], 1)
                dve.wait_ge(sm["prelude_chain"], b0 + J)
                stand(dve, "dve_go")
                for j in range(J):
                    dve.bn_aggr(mv[:, j, :], stats[:, j, :]).then_inc(sm["prelude_chain"], 1)
                dve.wait_ge(sm["std_ready"], g + 1)
                dve.reciprocal(rstd[:, :], std[:, :]).then_inc(sm["prelude_chain"], 1)
                dve.wait_ge(sm["prelude_chain"], b0 + 17)
                for j in range(J):
                    dve.tensor_scalar(y_v[:, j, :], emb(j), mv[:, j, 0:1], rstd[:, j:j + 1], ALU.subtract, ALU.mult
                                      ).then_inc(sm["prelude_chain"], 1)
                dve.wait_ge(sm["prelude_chain"], b0 + 25)
                for j in range(J):
                    ins = dve.tensor_tensor(res[:, ds(g, 1), j * H:(j + 1) * H].rearrange("p o h -> p (o h)"),
                                            emb(j), y_v[:, j, :], ALU.add)
                    ins.then_inc(sm["prelude_chain"], 1)
                dve.wait_ge(sm["prelude_chain"], b0 + 33)
                dve.sem_inc(sm["y_ready"], 1)
                for k in range(KC):
                    for q in range(2):
                        dve.wait_ge(sm["yT_ready"], 4 * g + 2 * k + q + 1)
                        dst = yT_v[:, k].rearrange("p (t j) -> p j t", j=J)[:, 4 * q:4 * q + 4]
                        dve.tensor_copy(dst, ps[:, (6 + 2 * k + q) % 8, :].rearrange("p (j t) -> p j t", j=4)
                                        ).then_inc(sm["yT_kept"], 1)
                dve.wait_ge(sm["q_kept"], 4 * g + 4)
                dve.wait_ge(sm["q_pieces_stored"], 12 * 16 * g)
                dve.tensor_copy(pieces[:, 0], q32_v).then_inc(sm["prelude_chain"], 1)
                dve.wait_ge(sm["prelude_chain"], b0 + 34)
                dve.tensor_tensor(r_v, q32_v, pieces[:, 0], ALU.subtract).then_inc(sm["prelude_chain"], 1)
                dve.wait_ge(sm["prelude_chain"], b0 + 35)
                dve.tensor_copy(pieces[:, 1], r_v).then_inc(sm["prelude_chain"], 1)
                dve.wait_ge(sm["prelude_chain"], b0 + 36)
                dve.tensor_tensor(pieces[:, 2], r_v, pieces[:, 1], ALU.subtract).then_inc(sm["q_pieces_ready"], 1)

            def reduce_step(m, t, gi):
                for u in range(4):
                    j, half, st = 2 * (t % 2) + u // 2, u % 2, t // 2
                    dve.wait_ge(sm["max_ready"], 4 * gi + u + 1)
                    col = 4 * j + st
                    dve.tensor_reduce(mx[:, ds(m % 2, 1), half, col:col + 1].rearrange("p o c -> p (o c)"),
                                      ps[:, MAX_BANK + u, :], AX.X, ALU.max).then_inc(sm["max_done"], 1)

            def combine(m):
                dve.wait_ge(sm["max_done"], 32 * (m + 1))
                dve.tensor_tensor(mxb[:, :], mx[:, ds(m % 2, 1), 0, :].rearrange("p o c -> p (o c)"),
                                  mx[:, ds(m % 2, 1), 1, :].rearrange("p o c -> p (o c)"), ALU.max).then_inc(sm["max_chain"], 1)
                dve.wait_ge(sm["max_chain"], 2 * m + 1)
                dve.tensor_scalar(mpc[:, 0:16], mxb[:, :], -1.0, None, ALU.mult).then_inc(sm["max_chain"], 1)
                dve.wait_ge(sm["max_chain"], 2 * m + 2)
                dve.scalar_tensor_tensor(out=mpc[:, 16:32], in0=mxb[:, :], scalar=-1.0, in1=mpc[:, 0:16],
                                         op0=ALU.mult, op1=ALU.subtract).then_inc(sm["mpc_ready"], 1)
                dve.wait_ge(sm["mpc_ready"], m + 1)
                dve.wait_ge(sm["m_loaded"], 128 * m)
                dve.transpose(mrow[:, :], mpc[:, :]).then_inc(sm["mrow_ready"], 1)

            with dve.Fori(0, NBLK) as m:
                for t in range(TT):
                    reduce_step(m, t, TT * m + t)
                combine(m)

            with dve.Fori(0, NTG) as g:
                n = [0]

                def mark(ins):
                    n[0] += 1
                    ins.then_inc(sm["t_chain"], 1)

                def link(ins):
                    mark(ins)
                    dve.wait_ge(sm["t_chain"], TC * g + n[0])

                resg = res[:, ds(g, 1)].rearrange("p o n -> p (o n)")
                num = y_v.rearrange("p j h -> p (j h)")
                den = yT_v.rearrange("p k t -> p (k t)")
                dve.wait_ge(sm["att_loaded"], 16 * 16 * (g + 1))
                link(dve.reciprocal(den, den))
                link(dve.tensor_tensor(num, num, den, ALU.mult))
                link(dve.tensor_tensor(resg, resg, num, ALU.add))
                hj = lambda j: res[:, ds(g, 1), j * H:(j + 1) * H].rearrange("p o h -> p (o h)")
                stand(dve, "dve_go")
                for j in range(J):
                    mark(dve.bn_stats(stats[:, j, :], hj(j)))
                dve.wait_ge(sm["t_chain"], TC * g + n[0])
                stand(dve, "dve_go")
                for j in range(J):
                    mark(dve.bn_aggr(mv[:, j, :], stats[:, j, :]))
                link(dve.tensor_copy(c1[:, :], tid[:, :]))
                assert n[0] == TA
                dve.wait_ge(sm["std_ready"], NTG + g + 1)
                link(dve.reciprocal(rstd[:, :], std[:, :]))
                dve.wait_ge(sm["scattered"], 16 * J * g)
                for j in range(J):
                    mark(dve.tensor_scalar(y2_v[:, j, :], hj(j), mv[:, j, 0:1], rstd[:, j:j + 1], ALU.subtract, ALU.mult))
                dve.wait_ge(sm["t_chain"], TC * g + n[0])
                dve.sem_inc(sm["t_std"], 1)
                for k in range(KC):
                    for q in range(2):
                        dve.wait_ge(sm["tT_ready"], 4 * g + 2 * k + q + 1)
                        if k == 0 and q == 0:
                            dve.wait_ge(sm["lg_ready"], g)
                        dve.tensor_copy(y2T_v[:, k, q * 512:(q + 1) * 512], ps[:, 2 * k + q, :]).then_inc(sm["tT_kept"], 1)
                dve.wait_ge(sm["lg_ready"], g + 1)
                lps = ps[:, 4, 0:J * E].rearrange("p (j e) -> p j e", j=J)
                link(dve.tensor_reduce(c1[:, :], lps, AX.X, ALU.max))
                link(dve.tensor_tensor(lg[:, :, :], lps, c1[:, :].unsqueeze(2).broadcast_to([P, J, E]), ALU.subtract))
                link(dve.tensor_scalar(run[:, :], eid[:, :], 1.0, None, ALU.mult))
                link(dve.tensor_scalar(slot[:, :], tid[:, :], 1.0, None, ALU.mult))
                link(dve.tensor_scalar(c3[:, :], tid[:, :], 1.0, None, ALU.mult))
                assert n[0] == TB, n[0]
                dve.wait_ge(sm["ex_ready"], g + 1)
                bj = lambda a: a[:, :].unsqueeze(2).broadcast_to([P, J, E])
                be_ = lambda a: a[:, :].unsqueeze(1).broadcast_to([P, J, E])
                link(dve.tensor_reduce(c2[:, :], ex[:, :, :], AX.X, ALU.add))
                link(dve.reciprocal(c3[:, :], c2[:, :]))
                link(dve.tensor_tensor(ex[:, :, :], ex[:, :, :], bj(c3), ALU.mult))
                link(dve.tensor_reduce(c1[:, :], ex[:, :, :], AX.X, ALU.max))
                link(dve.tensor_tensor(oh[:, :, :], ex[:, :, :], bj(c1), ALU.is_ge))
                link(dve.tensor_tensor(oh[:, :, :], oh[:, :, :], be_(rank8), ALU.mult))
                link(dve.tensor_reduce(c2[:, :], oh[:, :, :], AX.X, ALU.max))
                link(dve.tensor_tensor(oh[:, :, :], oh[:, :, :], bj(c2), ALU.is_equal))
                dve.tensor_reduce(cnt[:, :], oh[:, :, :].rearrange("p j e -> p e j"), AX.X, ALU.add).then_inc(sm["cnt_ready"], 1)
                dve.wait_ge(sm["pre_ready"], g + 1)
                link(dve.tensor_tensor(loc[:, 0, :], ps[:, 5, 0:E], base[:, :], ALU.add))
                for j in range(1, J):
                    link(dve.tensor_tensor(loc[:, j, :], loc[:, j - 1, :], oh[:, j - 1, :], ALU.add))
                link(dve.tensor_tensor(base[:, :], ps[:, 6, 0:E], base[:, :], ALU.add))
                link(dve.tensor_tensor(loc[:, :, :], loc[:, :, :], oh[:, :, :], ALU.mult))
                mark(dve.tensor_tensor(tmp[:, :, :], oh[:, :, :], be_(eid), ALU.mult))
                assert n[0] == TC - 2, n[0]
                dve.wait_ge(sm["t_chain"], TC * g + n[0])
                link(dve.tensor_reduce(c2[:, :], loc[:, :, :], AX.X, ALU.add))
                link(dve.tensor_reduce(c3[:, :], tmp[:, :, :], AX.X, ALU.add))
                assert n[0] == TC
                fn = [0]

                def flink(ins):
                    fn[0] += 1
                    ins.then_inc(sm["f_chain"], 1)
                    dve.wait_ge(sm["f_chain"], 7 * g + fn[0])

                flink(dve.tensor_scalar(kept[:, :], c2[:, :], float(CAP), None, ALU.is_lt))
                flink(dve.tensor_tensor(gates[:, ds(g, 1), :].rearrange("p o j -> p (o j)"), c1[:, :], kept[:, :], ALU.mult))
                flink(dve.scalar_tensor_tensor(out=slot[:, :], in0=c3[:, :], scalar=float(CAP), in1=c2[:, :],
                                               op0=ALU.mult, op1=ALU.add))
                flink(dve.tensor_tensor(slot[:, :], slot[:, :], kept[:, :], ALU.mult))
                flink(dve.tensor_copy(gidx[:, ds(g * J, J)], slot[:, :]))
                flink(dve.tensor_scalar(c2[:, :], kept[:, :], -1.0, 1.0, ALU.mult, ALU.add))
                flink(dve.tensor_tensor(c3[:, :], c2[:, :], tid[:, :], ALU.mult))
                dve.tensor_tensor(sidx[:, :], slot[:, :], c3[:, :], ALU.add).then_inc(sm["sidx_ready"], 1)
                dve.wait_ge(sm["sidx_ready"], g + 1)
                dve.tensor_scalar(tid[:, :], tid[:, :], float(TG), None, ALU.add).then_inc(sm["ohs"], 1)
                dve.wait_ge(sm["ohs"], g + 4)

            with dve.Fori(0, E) as e:
                dve.wait_ge(sm["eT_ready"], 3 * e + 1)
                dve.wait_ge(sm["e_ready"], 2 * e)
                dve.tensor_copy(We_T.rearrange("p c h -> p (c h)"), ps[:, 0, :]).then_inc(sm["eT_kept"], 1)
                for k in range(KC):
                    dve.wait_ge(sm["eT_ready"], 3 * e + 2 + k)
                    dve.tensor_copy(xe_T[:, k, :], ps[:, 1 + k, :]).then_inc(sm["eT_kept"], 1)
            with dve.Fori(0, NTG) as g:
                dve.tensor_copy(gateg[:, :], gates[:, ds(g, 1), :].rearrange("p o j -> p (o j)")).then_inc(sm["ohs"], 1)
                dve.wait_ge(sm["ohs"], 2 * NTG - NTG + 4 + g)
                dve.wait_ge(sm["gathered"], 16 * J * (g + 1))
                for j in range(J):
                    rj = res[:, ds(g, 1), j * H:(j + 1) * H].rearrange("p o h -> p (o h)")
                    dve.scalar_tensor_tensor(out=rj, in0=got[:, j, :], scalar=gateg[:, j:j + 1], in1=rj,
                                             op0=ALU.mult, op1=ALU.add).then_inc(sm["kv_sum"], 1)
                dve.wait_ge(sm["kv_sum"], 3 + J * (g + 1))
                dve.sem_inc(sm["final_ready"], 1)


_INS = ['x', 'L0_tok_U', 'L0_tok_s', 'L0_tok_Vt', 'L0_attn_keys', 'L0_attn_values', 'L0_attn_Wq_w', 'L0_attn_Wq_b',
        'L0_attn_Wk_w', 'L0_attn_Wk_b', 'L0_attn_Wv_w', 'L0_attn_Wv_b', 'L0_ffn_wg', 'L0_ffn_W', 'L0_ffn_b']


def kernel(**inputs):
    import numpy as _np
    import concourse.bacc as _bacc
    from concourse import mybir as _mybir
    from concourse.bass_utils import run_bass_kernel_spmd as _run

    nc = _bacc.Bacc("TRN2", target_bir_lowering=False, num_devices=1)
    arrays, args = {}, []
    for name in _INS:
        a = _np.ascontiguousarray(inputs[name])
        arrays[f"in_{name}"] = a
        args.append(nc.dram_tensor(f"in_{name}", a.shape, _mybir.dt.from_np(a.dtype), kind="ExternalInput").ap())
    args.append(nc.dram_tensor("out_h", (B * S, H), _mybir.dt.float32, kind="ExternalOutput").ap())
    build(nc, *args)
    r = _run(nc, [arrays], core_ids=[0])
    return r.results[0]["out_h"].reshape(B, S, H)
```

```python
from contextlib import ExitStack

import concourse.bass as bass
from concourse import mybir
from concourse.bass import ds

ALU = mybir.AluOpType
ACT = mybir.ActivationFunctionType
AX = mybir.AxisListType
F32 = mybir.dt.float32
BF16 = mybir.dt.bfloat16
I32 = mybir.dt.int32

P = 128
V, R = 25000, 64
H = 256
KC = H // P
B, S, T = 2, 2048, 1024
NH = 16
DH = H // NH
HG = 4
NG = NH // HG
SB = 512
NSB = S // SB
NBLK = B * NG * NSB
TT = T // P
J = 8
TG = P * J
NTG = B * S // TG
E = 8
CAP = B * S // E
EPS = 1e-5
SCALE = float(DH) ** -0.5
PIECES = (0, 0, 0, 1, 1, 2)
KPIECES = (0, 1, 2, 0, 1, 0)
KR = 16 * len(PIECES)
AHEAD = 13
PAY = 2 * H + 2
LAST = NBLK * TT
RING = 4


class Chain:

    def __init__(self, eng, sem):
        self.eng, self.sem, self.n = eng, sem, 0

    def mark(self, ins):
        ins.then_inc(self.sem, 1)
        self.n += 1
        return self.n

    def link(self, ins):
        self.mark(ins)
        self.eng.wait_ge(self.sem, self.n)


def build(nc, x, U, s_rank, Vt, keys, values, Wq_w, Wq_b, Wk_w, Wk_b, Wv_w, Wv_b, wg, We, be, out):
    with ExitStack() as ctx:
        def sb(name, shape, dt=F32):
            return ctx.enter_context(nc.sbuf_tensor(name, shape, dt))

        def sem(name):
            return ctx.enter_context(nc.semaphore(name))

        q_dram = nc.dram_tensor("q_dram", (3, NBLK, HG * DH, SB), BF16).ap()
        k_dram = nc.dram_tensor("k_dram", (3, H, T), BF16).ap()
        a_dram = nc.dram_tensor("a_dram", (NBLK, P, SB), F32).ap()
        xd_dram = nc.dram_tensor("xd_dram", (E * CAP, PAY), F32).ap()
        rd_dram = nc.dram_tensor("rd_dram", (NBLK, HG, SB), F32).ap()

        res = sb("res", [P, NTG, J * H])
        kst = sb("kst", [P, NH * T], BF16)
        qst = sb("qst", [P, 4, HG, SB], BF16)
        vaug = sb("vaug", [P, NG, TT * HG * 32])
        vblk = sb("vblk", [P, TT, HG, 32])
        probs_area = sb("probs_area", [P, 2 * J * PAY])
        probs = probs_area[:, 0:4 * RING * SB].rearrange("p (r s) -> p r s", s=2 * SB)
        acc = sb("acc", [P, 2, SB])
        ident = sb("ident", [P, P])
        identb = sb("identb", [P, P], BF16)
        upper = sb("upper", [P, P])
        ones = sb("ones", [P, P])
        mx = sb("mx", [P, 2, 2, 16])
        mxb = sb("mxb", [P, 16])
        mpc = sb("mpc", [P, 32], BF16)
        mrow = sb("mrow", [P, 32], BF16)
        idx = sb("idx", [P, NTG * J], I32)
        idxg = sb("idxg", [P, J], I32)
        srank = sb("srank", [R, 1])
        vt = sb("vt", [R, H])
        bq = sb("bq", [P, KC])
        bk = sb("bk", [P, KC])
        bv = sb("bv", [1, H])
        wgs = sb("wgs", [P, KC, E])
        early = sb("early", [P, 7680])
        wload = early[:, 0:1536].rearrange("p (w c h) -> p w c h", w=3, c=KC)
        wT = early[:, 1536:3072].rearrange("p (w c h) -> p w c h", w=3, c=KC)
        uT = early[0:R, 3072:4096]
        gemb = early[:, 4096:4608].rearrange("p (j r) -> p j r", j=J)
        pieces = early[:, 4608:7680].bitcast(BF16).rearrange("p (r c t) -> p r c t", r=3, c=KC)
        stats = sb("stats", [P, J, 6])
        mv = sb("mv", [P, J, 2])
        std = sb("std", [P, J])
        ri = sb("ri", [P, J], I32)
        rt = sb("rt", [P, J])
        rstd = sb("rstd", [P, 2, J])
        eidi = sb("eidi", [P, E], I32)
        eid = sb("eid", [P, E])
        rank8 = sb("rank8", [P, E])
        tidi = sb("tidi", [P, J], I32)
        tid = sb("tid", [P, J])
        lg = sb("lg", [P, J, E])
        ex = sb("ex", [P, J, E])
        oh = sb("oh", [P, J, E])
        loc = sb("loc", [P, J, E])
        tmp = sb("tmp", [P, J, E])
        c1 = sb("c1", [P, J])
        c2 = sb("c2", [P, J])
        c3 = sb("c3", [P, J])
        slot = sb("slot", [P, J])
        kept = sb("kept", [P, J])
        cnt = sb("cnt", [P, E])
        base = sb("base", [P, E])
        run = sb("run", [P, E])
        sidx = sb("sidx", [P, NTG, J], I32)
        pay_area = sb("pay_area", [P, 2 * J * PAY])
        oidx = sb("oidx", [P, 4, HG], I32)
        empty = sb("empty", [P, 4, HG])
        nmr = sb("nmr", [P, 2, J])

        def view(k):
            return probs[:, 2 * k:2 * k + 2, :].rearrange("p a b -> p (a b)")
        y_v = view(0).rearrange("p (j h) -> p j h", j=J)
        yT_v = view(1).rearrange("p (k t) -> p k t", k=KC)
        q32_v = view(2).rearrange("p (k t) -> p k t", k=KC)
        r_v = view(3).rearrange("p (k t) -> p k t", k=KC)
        kv_load = y_v
        kst32 = kst[:, :].bitcast(F32)
        flat = probs[:, :, :].rearrange("p a b -> p (a b)")
        pay = [a[:, n * J * PAY:(n + 1) * J * PAY].rearrange("p (j h) -> p j h", j=J)
               for a in (pay_area, probs_area) for n in range(2)]
        x_load = [p[:, 0:HG] for p in pay]
        num = [early[:, 0:2048], early[:, 2048:4096]]
        rden = early[:, 4096:4608]
        rdb = [early[:, 4608:6656], vaug[:, 0:2].rearrange("p a b -> p (a b)")]
        y2T = [a.rearrange("p (k t) -> p k t", k=KC) for a in
               [rdb[0]] + 3 * [vaug[:, 2:4].rearrange("p a b -> p (a b)")]]
        xe_T = [vaug[:, 2 + n].rearrange("p (c t) -> p c t", c=KC) for n in range(2)]
        we_load = kst32[:, 0:4096].rearrange("p (e c h) -> p e c h", e=E, c=KC)
        we_T = kst32[:, 4096:8192].rearrange("p (e n) -> p e n", e=E)
        flat = res[:, :, :].rearrange("p g n -> p (g n)")
        y_out = flat[:, 0:4096].rearrange("p (e n h) -> p e n h", e=4, n=HG)
        y_sum = flat[:, 4096:6144].rearrange("p (e n h) -> p e n h", e=2, n=HG)
        bb = flat[:, 6144:7168].rearrange("p (e h) -> p e h", e=4)
        we_now = flat[:, 7168:8192].rearrange("p (e n) -> p e n", e=2)
        eps_t = sb("eps_t", [P, 1])

        ps = ctx.enter_context(nc.psum_tensor("ps", [P, 8, 512], F32))
        MAX_BANK, PV_BANK = 3, 7
        EXP_BANK = (0, 1, 2, 1)
        EXP_BACK = (4, 2, 4, 2)

        names = """w_loaded c_loaded kv_loaded idx_loaded const_made wT_ready wT_kept kvT_ready kvT_kept
            proj_ready proj_kept kv_sum pieces_ready pieces_stored k_stacked ones_set
            idx_picked rows_gathered uT_ready uT_kept emb_ready y_ready yT_ready yT_kept q_ready q_kept
            std_ready q_pieces_ready q_pieces_stored prelude_chain
            q_loaded va_loaded vb_loaded scores_ready exp_done pv_done max_ready max_done max_chain
            mpc_ready mrow_ready m_loaded acc_ready acc_stored
            zeroed att_loaded0 att_loaded1 att_loaded2 att_loaded3 t_chain y2_ready tT_ready tT_kept lg_ready
            lg_shifted ex_ready cnt_ready pre_ready sidx_ready scattered x_loaded0 x_loaded1 x_loaded2 x_loaded3
            xT_ready xT_kept e_ready0 e_ready1 y_free0 y_free1 e_chain y_chain y_out_ready we_kept
            out_stored0 out_stored1 out_stored2 out_stored3 base_stored den_loaded we_loaded rden_ready rden_stored
            h2_ready num_scaled weT_ready weT_kept rstd_ready zset p_chain ohs sp_go pool_go pe_go dve_go""".split()
        sm = {n: sem(n) for n in names}

        def stand(eng, name):
            eng.sem_inc(sm[name], 1)

        block = ctx.enter_context(nc.Block())

        @block.sync
        def _(sp):
            for n, w in enumerate((Wq_w, Wk_w, Wv_w)):
                sp.dma_start(wload[:, n], w.rearrange("(c p) h -> p c h", p=P)).then_inc(sm["w_loaded"], 16)
            sp.dma_start(idx[:, :].rearrange("p (b h j) -> p b h j", b=B, j=J),
                         x.rearrange("b (h p j) -> p b h j", p=P, j=J)).then_inc(sm["idx_loaded"], 16)
            sp.dma_start(kv_load, keys.rearrange("o (n p) h -> p (o n) h", p=P)).then_inc(sm["kv_loaded"], 16)
            sp.dma_start(bq[:, :], Wq_b.rearrange("(c p) -> p c", p=P), allow_slow_non_contiguous=True).then_inc(sm["c_loaded"], 16)
            sp.dma_start(bk[:, :], Wk_b.rearrange("(c p) -> p c", p=P), allow_slow_non_contiguous=True).then_inc(sm["c_loaded"], 16)
            sp.dma_start(bv[:, :], Wv_b.rearrange("(o h) -> o h", o=1)).then_inc(sm["c_loaded"], 16)
            sp.dma_start(srank[:, :], s_rank.rearrange("(r o) -> r o", o=1), allow_slow_non_contiguous=True).then_inc(sm["c_loaded"], 16)
            sp.dma_start(vt[:, :], Vt).then_inc(sm["c_loaded"], 16)
            sp.dma_start(wgs[:, :, :], wg.rearrange("(c p) e -> p c e", p=P)).then_inc(sm["c_loaded"], 16)
            sp.wait_ge(sm["zset"], 1)
            for n in range(8):
                sp.dma_start(xd_dram[n * CAP:(n + 1) * CAP, :].rearrange("(p j) h -> p (j h)", p=P),
                             pay[0][:, 0:4].rearrange("p j h -> p (j h)")).then_inc(sm["zeroed"], 16)
            sp.wait_ge(sm["pieces_ready"], 1)
            for r in range(3):
                sp.dma_start(k_dram[r].rearrange("(c p) t -> p c t", p=P), pieces[:, r]).then_inc(sm["pieces_stored"], 16)
            sp.wait_ge(sm["kvT_ready"], 4)
            sp.dma_start(kv_load, values.rearrange("o (n p) h -> p (o n) h", p=P)).then_inc(sm["kv_loaded"], 16)
            sp.wait_ge(sm["pieces_stored"], 48)
            for r, pc in enumerate(KPIECES):
                sp.dma_start(kst[16 * r:16 * r + 16, :].rearrange("p (h t) -> p h t", h=NH),
                             k_dram[pc].rearrange("(h i) t -> i h t", i=DH)).then_inc(sm["k_stacked"], 16)
            with sp.Fori(0, NTG) as g:
                sp.wait_ge(sm["q_pieces_ready"], g + 1)
                stand(sp, "sp_go")
                for r in range(3):
                    for c in range(KC):
                        for hh in range(2):
                            dst = q_dram[r, ds((g // 2) * 16 + (g % 2) * 2 + (2 * c + hh) * 4, 2)]
                            sp.dma_start(dst.rearrange("n p s -> p n s"),
                                         pieces[64 * hh:64 * hh + 64, r, c].rearrange("p (n s) -> p n s", n=2)
                                         ).then_inc(sm["q_pieces_stored"], 16)
            sp.wait_ge(sm["q_pieces_stored"], NTG * 12 * 16)

            def load_q(i):
                for r, pc in enumerate(PIECES):
                    sp.dma_start(qst[16 * r:16 * r + 16, ds(i % 4, 1)].rearrange("p o j s -> p (o j) s"),
                                 q_dram[pc, ds(i, 1)].rearrange("o (j i) s -> (o i) j s", i=DH)
                                 ).then_inc(sm["q_loaded"], 16)

            def load_v(i, half):
                n = HALF_V
                sp.dma_start(vblk[:, 4 * half:4 * half + 4].rearrange("p t j c -> p (t j c)"),
                             vaug[:, ds((i // NSB) % NG, 1), half * n:(half + 1) * n].rearrange("p o n -> p (o n)")
                             ).then_inc(sm["vb_loaded" if half else "va_loaded"], 16)

            def load_m(i):
                sp.wait_ge(sm["mrow_ready"], i + 1)
                for c in range(2):
                    row = qst[KR + c:KR + c + 1, ds(i % 4, 1)].rearrange("p o j (t q s) -> p (o j t) q s", q=4, s=32)
                    for q in range(4):
                        sp.dma_start(row[:, :, q, :], mrow[32 * q + 16 * c:32 * q + 16 * c + 16, :]
                                     ).then_inc(sm["m_loaded"], 16)

            HALF_V = 4 * HG * 32
            sp.wait_ge(sm["ones_set"], 2)
            sp.wait_ge(sm["proj_kept"], 8)
            for i in range(3):
                load_q(i)
                if i < 2:
                    sp.wait_ge(sm["q_loaded"], 96 * (i + 1))
            load_v(0, 0)
            load_m(0)

            def store_acc(i):
                sp.wait_ge(sm["acc_ready"], i + 1)
                sp.dma_start(a_dram[ds(i, 1)].rearrange("o p s -> (o p) s"),
                             acc[:, ds(i % 2, 1)].rearrange("p o s -> p (o s)")).then_inc(sm["acc_stored"], 16)

            def block_sp(i, first=False, more_q=True, more=True, mid=None, end=None):
                sp.wait_ge(sm["pv_done"], TT * i)
                load_v(i, 1)
                if not first:
                    store_acc(i - 1)
                if more_q:
                    sp.wait_ge(sm["scores_ready"], HG * TT * i)
                    sp.wait_ge(sm["q_loaded"], 96 * (i + 3))
                    load_q(i + 3)
                if more:
                    load_m(i + 1)
                    if mid:
                        mid()
                    sp.wait_ge(sm["pv_done"], TT * i + 4)
                    load_v(i + 1, 0)
                if end:
                    end()

            block_sp(0, first=True)
            with sp.Fori(0, (NBLK - 6) // 2) as u:
                for par in range(2):
                    block_sp(2 * u + par + 1)

            def load_den(b):
                n = NBLK // B
                sp.wait_ge(sm["acc_stored"], 16 * n * (b + 1))
                sp.dma_start(rden[64 * b:64 * b + 64], a_dram[n * b:n * (b + 1)].rearrange("n (j y) s -> (n j) y s", j=HG)[:, DH]
                             ).then_inc(sm["den_loaded"], 16)

            def store_rden(b):
                n = NBLK // B
                sp.wait_ge(sm["rden_ready"], b + 1)
                sp.dma_start(rd_dram[n * b:n * (b + 1)].rearrange("n j s -> (n j) s"), rden[64 * b:64 * b + 64]
                             ).then_inc(sm["rden_stored"], 16)

            def load_att(g):
                for q in range(2):
                    for j in range(HG):
                        p0 = 64 * q + DH * j
                        n0 = 8 * g + 4 * q
                        sp.dma_start(num[g % 2][p0:p0 + DH].rearrange("p (n s) -> p n s", n=4),
                                     a_dram[n0:n0 + 4, 32 * j:32 * j + DH].rearrange("n x s -> x n s")
                                     ).then_inc(sm[f"att_loaded{g}"], 16)
                if g != 1:
                    sp.wait_ge(sm["rden_stored"], 16 * (g // 2 + 1))
                for q in range(2):
                    for j in range(HG):
                        p0 = 64 * q + DH * j
                        n0 = 8 * g + 4 * q
                        sp.dma_start(rdb[g % 2][p0:p0 + DH].rearrange("p (n s) -> p n s", n=4),
                                     rd_dram[n0:n0 + 4, j].unsqueeze(0).broadcast_to([DH, 4, SB])
                                     ).then_inc(sm[f"att_loaded{g}"], 16)

            def store_base(g):
                sp.wait_ge(sm["h2_ready"], g + 1)
                sp.dma_start(out[g * TG:(g + 1) * TG].rearrange("(p j) h -> p j h", p=P), pay[g][:, :, H:2 * H]
                             ).then_inc(sm["base_stored"], 16)

            def att0():
                store_rden(0)
                load_att(0)

            def att1():
                sp.wait_ge(sm["vb_loaded"], 16 * (NBLK - 2))
                load_att(1)

            def bases():
                store_base(0)
                store_base(1)

            block_sp(NBLK - 5)
            block_sp(NBLK - 4, end=lambda: load_den(0))
            block_sp(NBLK - 3, more_q=False, mid=att0, end=att1)
            block_sp(NBLK - 2, more_q=False)
            block_sp(NBLK - 1, more_q=False, more=False, end=bases)
            store_acc(NBLK - 1)
            load_den(1)
            sp.wait_ge(sm["pv_done"], TT * NBLK)
            sp.wait_ge(sm["num_scaled"], 2)
            store_rden(1)
            sp.wait_ge(sm["lg_ready"], 1)
            load_att(2)
            sp.dma_start(we_load, We.rearrange("e (c p) h -> p e c h", p=P)).then_inc(sm["we_loaded"], 16)
            load_att(3)
            store_base(2)
            store_base(3)

            sp.wait_ge(sm["scattered"], NTG * J * 16)

            def load_expert(e, par):
                sp.dma_start(x_load[par], xd_dram[ds(e * CAP, CAP)].rearrange("(n p) h -> p n h", p=P)
                             ).then_inc(sm[f"x_loaded{par}"], 16)
                sp.dma_start(bb[:, par], be[ds(e, 1)].broadcast_to([P, H])).then_inc(sm[f"x_loaded{par}"], 16)

            sp.wait_ge(sm["base_stored"], NTG * 16)
            for par in range(4):
                load_expert(par, par)
            for par in range(4):
                sp.wait_ge(sm["y_out_ready"], par + 1)
                load_expert(par + 4, par)

        @block.gpsimd
        def _(pool):
            ch = Chain(pool, sm["p_chain"])
            ch.link(pool.memset(ident[:, :], 0.0))
            ch.link(pool.memset(upper[:, :], 1.0))
            ch.link(pool.affine_select(out=ident[:, :], in_=ident[:, :], compare_op=ALU.not_equal, fill=1.0,
                                       base=0, pattern=[[-1, P]], channel_multiplier=1))
            ch.link(pool.affine_select(out=upper[:, :], in_=upper[:, :], compare_op=ALU.is_gt, fill=0.0,
                                       base=0, pattern=[[1, P]], channel_multiplier=-1))
            ch.link(pool.iota(eidi[:, :], [[1, E]], 0, 0))
            ch.link(pool.iota(tidi[:, :], [[1, J]], 1, J))
            ch.link(pool.tensor_copy(identb[:, :], ident[:, :]))
            ch.link(pool.tensor_copy(eid[:, :], eidi[:, :]))
            ch.link(pool.tensor_copy(tid[:, :], tidi[:, :]))
            pool.tensor_scalar(rank8[:, :], eid[:, :], -1.0, float(E), ALU.mult, ALU.add).then_inc(sm["const_made"], 1)
            pool.wait_ge(sm["idx_loaded"], 16)
            with pool.Fori(0, NTG) as g:
                pool.wait_ge(sm["rows_gathered"], 16 * J * g)
                pool.tensor_copy(idxg[:, :], idx[:, ds(g * J, J)]).then_inc(sm["idx_picked"], 1)
                pool.wait_ge(sm["idx_picked"], g + 1)
                pool.wait_ge(sm["uT_ready"], 2 * g)
                stand(pool, "pool_go")
                for j in range(J):
                    pool.indirect_dma_start(gemb[:, j], None, U, bass.IndirectOffsetOnAxis(ap=idxg[:, j:j + 1], axis=0)
                                            ).then_inc(sm["rows_gathered"], 16)
            for g in range(2):
                pool.wait_ge(sm[f"att_loaded{g}"], 16 * 16)
                pool.tensor_tensor(num[g], num[g], rdb[g], ALU.mult).then_inc(sm["num_scaled"], 1)
                pool.wait_ge(sm["num_scaled"], g + 1)
                pool.tensor_tensor(pay[g][:, :, H:2 * H], res[:, g].rearrange("p (j h) -> p j h", j=J),
                                   num[g].rearrange("p (j h) -> p j h", j=J), ALU.add).then_inc(sm["h2_ready"], 1)
            pool.wait_ge(sm["zeroed"], 16 * E)
            for g in range(NTG):
                pool.wait_ge(sm["sidx_ready"], g + 1)
                for j in range(J):
                    pool.indirect_dma_start(
                        xd_dram, bass.IndirectOffsetOnAxis(ap=sidx[:, g, j:j + 1], axis=0), pay[g][:, j], None,
                        bounds_check=E * CAP - 1, oob_is_err=False).then_inc(sm["scattered"], 16)
            pool.wait_ge(sm["base_stored"], 16 * NTG)
            with pool.Fori(0, E // 4) as u:
                for par in range(4):
                    pool.wait_ge(sm["y_out_ready"], 4 * u + par + 1)
                    stand(pool, "pool_go")
                    for n in range(4):
                        pool.indirect_dma_start(
                            out, bass.IndirectOffsetOnAxis(ap=oidx[:, par, n:n + 1], axis=0), y_out[:, par, n], None,
                            bounds_check=B * S - 1, oob_is_err=False).then_inc(sm[f"out_stored{par}"], 16)
            for par in range(4):
                pool.wait_ge(sm[f"out_stored{par}"], 16 * E)

        @block.tensor
        def _(pe):
            pe.wait_ge(sm["w_loaded"], 48)
            pe.wait_ge(sm["const_made"], 1)
            for w in range(3):
                for k in range(KC):
                    for c in range(KC):
                        mm = pe.transpose(ps[:, w, (k * KC + c) * P:(k * KC + c + 1) * P],
                                          wload[:, w, c, k * P:(k + 1) * P], ident[:, :])
                mm.then_inc(sm["wT_ready"], 1)

            def turn_kv(bank, first):
                for k in range(KC):
                    for q in range(2):
                        if not first:
                            pe.wait_ge(sm["kvT_kept"], 4)
                        for n in range(4):
                            mm = pe.transpose(ps[:, bank + 2 * k + q, n * P:(n + 1) * P],
                                              kv_load[:, 4 * q + n, k * P:(k + 1) * P], ident[:, :])
                        mm.then_inc(sm["kvT_ready"], 1)

            pe.wait_ge(sm["kv_loaded"], 16)
            turn_kv(3, True)
            pe.wait_ge(sm["wT_kept"], 3)
            pe.wait_ge(sm["kvT_kept"], 4)
            for c in range(KC):
                for n in range(2):
                    for k in range(KC):
                        mm = pe.matmul(ps[:, 3 + 2 * c + n, :], wT[:, 1, k, c * P:(c + 1) * P],
                                       yT_v[:, k, n * 512:(n + 1) * 512], start=(k == 0), stop=(k == 1))
                    mm.then_inc(sm["proj_ready"], 1)
            pe.wait_ge(sm["kv_loaded"], 32)
            pe.wait_ge(sm["proj_kept"], 4)
            turn_kv(3, False)
            pe.wait_ge(sm["kvT_kept"], 8)
            pe.wait_ge(sm["c_loaded"], 6 * 16)
            pe.wait_ge(sm["ohs"], 1)
            for n in range(TT):
                o = ps[:, 3 + n // 2, (n % 2) * H:(n % 2 + 1) * H]
                for k in range(KC):
                    pe.matmul(o, yT_v[:, k, n * P:(n + 1) * P], wT[:, 2, k, :], start=(k == 0), stop=False)
                mm = pe.matmul(o, ones[0:1, :], bv[:, :], start=False, stop=True)
                if n % 2:
                    mm.then_inc(sm["proj_ready"], 1)
            pe.wait_ge(sm["proj_kept"], 8)
            with pe.Fori(0, NTG) as g:
                pe.wait_ge(sm["rows_gathered"], 16 * J * (g + 1))
                pe.wait_ge(sm["yT_kept"], 4 * g)
                stand(pe, "pe_go")
                for q in range(2):
                    for n in range(4):
                        mm = pe.transpose(ps[0:R, q, n * P:(n + 1) * P], gemb[:, 4 * q + n, :], ident[:, :])
                    mm.then_inc(sm["uT_ready"], 1)
                pe.wait_ge(sm["uT_kept"], 2 * g + 2)
                pe.wait_ge(sm["q_kept"], 4 * g)
                for j in range(J):
                    mm = pe.matmul(ps[:, 2 + j // 2, (j % 2) * H:(j % 2 + 1) * H], uT[:, j * P:(j + 1) * P], vt[:, :],
                                   start=True, stop=True)
                mm.then_inc(sm["emb_ready"], 1)
                pe.wait_ge(sm["y_ready"], g + 1)
                for k in range(KC):
                    for q in range(2):
                        for n in range(4):
                            mm = pe.transpose(ps[:, (6 + 2 * k + q) % 8, n * P:(n + 1) * P],
                                              y_v[:, 4 * q + n, k * P:(k + 1) * P], ident[:, :])
                        mm.then_inc(sm["yT_ready"], 1)
                pe.wait_ge(sm["yT_kept"], 4 * g + 4)
                for c in range(KC):
                    for n in range(2):
                        for k in range(KC):
                            mm = pe.matmul(ps[:, 2 + 2 * c + n, :], wT[:, 0, k, c * P:(c + 1) * P],
                                           yT_v[:, k, n * 512:(n + 1) * 512], start=(k == 0), stop=(k == 1))
                        mm.then_inc(sm["q_ready"], 1)

            pe.wait_ge(sm["k_stacked"], 6 * 16)
            pe.wait_ge(sm["ones_set"], 2)
            pe.wait_ge(sm["q_kept"], 4 * NTG)
            pe.wait_ge(sm["const_made"], 1)

            def maximum(m, t, gi, u):
                if t == 0 and u == 0:
                    pe.wait_ge(sm["q_loaded"], 96 * (m + 1))
                hg = (m // NSB) % NG
                j, half, st = 2 * (t % 2) + u // 2, u % 2, t // 2
                if not (isinstance(gi, int) and gi == 0):
                    pe.wait_ge(sm["max_done"], 4 * gi + u - 3)
                pe.matmul(ps[:, MAX_BANK + u, :],
                          qst[0:KR, ds(m % 4, 1), j, st * P:(st + 1) * P].rearrange("p o s -> p (o s)"),
                          kst[0:KR, ds((hg * HG + j) * T + half * 512, 512)],
                          start=True, stop=True).then_inc(sm["max_ready"], 1)

            def score(i, t, j):
                hg = (i // NSB) % NG
                n = HG * TT * i + HG * t + j + 1 - EXP_BACK[j]
                if not (isinstance(n, int) and n < 1):
                    pe.wait_ge(sm["exp_done"], n)
                pe.matmul(ps[:, EXP_BANK[j], :], kst[0:KR + 2, ds((hg * HG + j) * T + t * P, P)],
                          qst[0:KR + 2, ds(i % 4, 1), j, :].rearrange("p o s -> p (o s)"),
                          start=True, stop=True).then_inc(sm["scores_ready"], 1)

            def pv(i, t):
                pe.wait_ge(sm["exp_done"], HG * (TT * i + t + 1))
                if t == 0:
                    pe.wait_ge(sm["va_loaded"], 16 * (i + 1))
                    pe.wait_ge(sm["acc_ready"], i)
                if t == 4:
                    pe.wait_ge(sm["vb_loaded"], 16 * (i + 1))
                for j in range(HG):
                    mm = pe.matmul(ps[32 * j:32 * j + 32, PV_BANK, :], vblk[:, t, j, :],
                                   probs[:, 2 * (t % RING) + j // 2, (j % 2) * SB:(j % 2 + 1) * SB],
                                   start=(t == 0), stop=(t == TT - 1))
                mm.then_inc(sm["pv_done"], 1)

            def block_pe(i, first=False, ahead=TT, extra={}):
                pe.wait_ge(sm["m_loaded"], 128 * (i + 1))
                for t in range(TT):
                    far = t + AHEAD
                    if t in extra:
                        extra[t]()
                    for step in "s0 m0 s1 s2 m1 pv s3 m2 m3".split():
                        if step[0] == "s":
                            score(i, t, int(step[1]))
                        elif step == "pv":
                            if t:
                                pv(i, t - 1)
                            elif not first:
                                pv(i - 1, TT - 1)
                        elif t < ahead:
                            maximum(i + far // TT, far % TT, TT * i + far, int(step[1]))

            for gi in range(AHEAD):
                for u in range(4):
                    maximum(gi // TT, gi % TT, gi, u)
            block_pe(0, first=True)
            with pe.Fori(0, (NBLK - 4) // 2) as u:
                for par in range(2):
                    block_pe(2 * u + par + 1)
            block_pe(NBLK - 3)
            block_pe(NBLK - 2, ahead=2 * TT - AHEAD)

            TURN_BANK = ((3, 4, 5, 6), (0, 1, 2, 4), (3, 5, 6, 7), (0, 1, 2, 4))

            def turn_y2(g):
                pe.wait_ge(sm["y2_ready"], g + 1)
                for k in range(KC):
                    for q in range(2):
                        for n in range(4):
                            mm = pe.transpose(ps[:, TURN_BANK[g][2 * k + q], n * P:(n + 1) * P],
                                              pay[g][:, 4 * q + n, k * P:(k + 1) * P], ident[:, :])
                        mm.then_inc(sm["tT_ready"], 1)

            def logits(g):
                pe.wait_ge(sm["tT_kept"], 4 * g + 4)
                for j in range(J):
                    for k in range(KC):
                        mm = pe.matmul(ps[:, TURN_BANK[g][0], j * E:(j + 1) * E], y2T[g][:, k, j * P:(j + 1) * P], wgs[:, k, :],
                                       start=(k == 0), stop=(k == 1))
                mm.then_inc(sm["lg_ready"], 1)

            def prefix(g):
                pe.wait_ge(sm["cnt_ready"], g + 1)
                bank = TURN_BANK[g][0]
                pe.matmul(ps[:, bank, 64:64 + E], upper[:, :], cnt[:, :], start=True, stop=True)
                pe.matmul(ps[:, bank, 80:80 + E], ones[:, :], cnt[:, :], start=True, stop=True).then_inc(sm["pre_ready"], 1)

            def turn_we(experts):
                for e in experts:
                    if e >= 3:
                        pe.wait_ge(sm["weT_kept"], e - 2)
                    for k in range(KC):
                        for c in range(KC):
                            mm = pe.transpose(ps[:, 5 + e % 3, (k * KC + c) * P:(k * KC + c + 1) * P],
                                              we_load[:, e, c, k * P:(k + 1) * P], ident[:, :])
                    mm.then_inc(sm["weT_ready"], 1)

            def last_maxima():
                pe.wait_ge(sm["max_done"], 4 * LAST)
                turn_y2(0)

            block_pe(NBLK - 1, ahead=0, extra={1: last_maxima, 4: lambda: logits(0), 7: lambda: prefix(0)})
            pv(NBLK - 1, TT - 1)
            pe.wait_ge(sm["exp_done"], HG * TT * NBLK)
            turn_y2(1)
            logits(1)
            prefix(1)
            pe.wait_ge(sm["acc_ready"], NBLK)
            pe.wait_ge(sm["sidx_ready"], 1)
            turn_y2(2)
            logits(2)
            pe.wait_ge(sm["we_loaded"], 16)
            turn_we((0, 1, 2))
            pe.wait_ge(sm["sidx_ready"], 2)
            turn_y2(3)
            logits(3)
            prefix(2)
            turn_we((3, 4, 5))
            prefix(3)
            turn_we((6, 7))
            pe.wait_ge(sm["weT_kept"], E)
            pe.wait_ge(sm["sidx_ready"], NTG)

            with pe.Fori(0, E // 4) as u:
                for par in range(4):
                    e, half = 4 * u + par, par % 2
                    pe.wait_ge(sm[f"y_free{half}"], 2 * u + par // 2 + 1)
                    pe.wait_ge(sm[f"x_loaded{par}"], 32 * u + 32)
                    for k in range(KC):
                        for n in range(4):
                            mm = pe.transpose(ps[:, 2 * half + k, n * P:(n + 1) * P], x_load[par][:, n, k * P:(k + 1) * P],
                                              ident[:, :])
                        mm.then_inc(sm["xT_ready"], 1)
                    pe.wait_ge(sm["we_kept"], e + 1)
                    pe.wait_ge(sm["xT_kept"], 2 * e + 2)
                    for n in range(4):
                        o = ps[:, 4 + 2 * half + n // 2, (n % 2) * H:(n % 2 + 1) * H]
                        for k in range(KC):
                            mm = pe.matmul(o, xe_T[half][:, k, n * P:(n + 1) * P], we_now[:, half, k * H:(k + 1) * H],
                                           start=(k == 0), stop=(k == 1))
                        if n % 2:
                            mm.then_inc(sm[f"e_ready{half}"], 1)

        @block.scalar
        def _(act):
            act.wait_ge(sm["c_loaded"], 6 * 16)
            for n in range(4):
                act.wait_ge(sm["proj_ready"], n + 1)
                act.activation(q32_v[:, n // 2, (n % 2) * 512:(n % 2 + 1) * 512], ps[:, 3 + n, :], ACT.Relu,
                               bias=bk[:, n // 2:n // 2 + 1]).then_inc(sm["proj_kept"], 1)
            act.wait_ge(sm["ones_set"], 1)
            for n in range(4):
                act.wait_ge(sm["proj_ready"], 5 + n)
                for u in range(2):
                    tt = 2 * n + u
                    dst = vaug[:, :, :].rearrange("p g (t j c) -> p g t j c", t=TT, j=HG)[:, :, tt, :, 0:DH]
                    ins = act.activation(dst, ps[:, 3 + n, u * H:(u + 1) * H].rearrange("p (g j c) -> p g j c", g=NG, j=HG),
                                         ACT.Relu)
                ins.then_inc(sm["proj_kept"], 1)
            with act.Fori(0, NTG) as g:
                act.wait_ge(sm["prelude_chain"], 36 * g + 16)
                act.activation(std[:, :], mv[:, :, 1], ACT.Sqrt, bias=eps_t[:, 0:1]).then_inc(sm["std_ready"], 1)
                act.wait_ge(sm["q_pieces_ready"], g)
                for n in range(4):
                    act.wait_ge(sm["q_ready"], 4 * g + n + 1)
                    act.activation(q32_v[:, n // 2, (n % 2) * 512:(n % 2 + 1) * 512], ps[:, 2 + n, :], ACT.Relu,
                                   bias=bq[:, n // 2:n // 2 + 1]).then_inc(sm["q_kept"], 1)
            act.wait_ge(sm["q_pieces_ready"], NTG)

            def exps(i, t, first=False):
                for j in range(HG):
                    act.wait_ge(sm["scores_ready"], HG * (TT * i + t) + j + 1)
                    if not (isinstance(i, int) and i == 0 and t < RING) and j == 0:
                        act.wait_ge(sm["pv_done"], TT * i + t - RING + 1)
                    act.activation(probs[:, 2 * (t % RING) + j // 2, (j % 2) * SB:(j % 2 + 1) * SB],
                                   ps[:, EXP_BANK[j], :], ACT.Exp, scale=SCALE).then_inc(sm["exp_done"], 1)
                    if j == HG - 2 and t == 0 and not first:
                        keep_acc(i - 1)

            def keep_acc(i):
                act.wait_ge(sm["pv_done"], TT * (i + 1))
                if not (isinstance(i, int) and i < 2):
                    act.wait_ge(sm["acc_stored"], 16 * (i - 1))
                act.activation(acc[:, ds(i % 2, 1)].rearrange("p o s -> p (o s)"), ps[:, PV_BANK, :], ACT.Copy
                               ).then_inc(sm["acc_ready"], 1)

            def shares(g):
                act.wait_ge(sm["lg_shifted"], g + 1)
                act.activation(ex[:, :, :], lg[:, :, :], ACT.Exp).then_inc(sm["ex_ready"], 1)

            def block_act(i, first=False, extra={}):
                for t in range(TT):
                    if t in extra:
                        extra[t]()
                    exps(i, t, first)

            block_act(0, first=True)
            block_act(1)
            with act.Fori(1, NBLK // 2 - 1) as u:
                for par in range(2):
                    block_act(2 * u + par)
            block_act(NBLK - 2)
            block_act(NBLK - 1, extra={6: lambda: shares(0)})
            keep_acc(NBLK - 1)

            def norm_act(g):
                act.wait_ge(sm["rstd_ready"], g + 1)
                for j in range(J):
                    ins = act.activation(pay[g][:, j, 0:H], pay[g][:, j, H:2 * H], ACT.Identity,
                                         bias=nmr[:, g % 2, j:j + 1], scale=rstd[:, g % 2, j:j + 1])
                ins.then_inc(sm["y2_ready"], 1)

            def keep_y2(g):
                act.wait_ge(sm["lg_ready"], g)
                for n in range(4):
                    act.wait_ge(sm["tT_ready"], 4 * g + n + 1)
                    act.activation(y2T[g][:, n // 2, (n % 2) * 512:(n % 2 + 1) * 512], ps[:, ((0, 1, 2, 4), (3, 5, 6, 7))[g == 2][n], :],
                                   ACT.Copy).then_inc(sm["tT_kept"], 1)

            def keep_we(experts):
                for e in experts:
                    act.wait_ge(sm["weT_ready"], e + 1)
                    act.activation(we_T[:, e], ps[:, 5 + e % 3], ACT.Copy).then_inc(sm["weT_kept"], 1)

            keep_y2(1)
            shares(1)
            norm_act(2)
            keep_y2(2)
            keep_we((0, 1, 2))
            norm_act(3)
            keep_y2(3)
            shares(2)
            keep_we((3, 4, 5))
            shares(3)
            keep_we((6, 7))
            with act.Fori(0, E // 4) as u:
                for par in range(4):
                    e, half = 4 * u + par, par % 2
                    act.wait_ge(sm[f"e_ready{half}"], 2 * (2 * u + par // 2))
                    act.activation(we_now[:, half], we_T[:, ds(e, 1)].rearrange("p o n -> p (o n)"), ACT.Copy
                                   ).then_inc(sm["we_kept"], 1)
                    for k in range(KC):
                        act.wait_ge(sm["xT_ready"], 2 * e + k + 1)
                        act.activation(xe_T[half][:, k], ps[:, 2 * half + k], ACT.Copy).then_inc(sm["xT_kept"], 1)

        @block.vector
        def _(dve):
            dve.memset(pay[0][:, 0:4].rearrange("p j h -> p (j h)"), 0.0).then_inc(sm["zset"], 1)
            dve.memset(vaug[:, :, :], 1.0).then_inc(sm["ones_set"], 1)
            dve.memset(ones[:, :], 1.0).then_inc(sm["ohs"], 1)
            dve.memset(eps_t[:, :], EPS).then_inc(sm["ohs"], 1)
            dve.memset(base[:, :], 0.0).then_inc(sm["ohs"], 1)
            for w in range(3):
                dve.wait_ge(sm["wT_ready"], w + 1)
                dve.tensor_copy(wT[:, w].rearrange("p c h -> p (c h)"), ps[:, w, :]).then_inc(sm["wT_kept"], 1)

            def keep_kv(n0):
                for n in range(4):
                    dve.wait_ge(sm["kvT_ready"], n0 + n + 1)
                    if n0:
                        dve.wait_ge(sm["proj_ready"], 4)
                    dve.tensor_copy(yT_v[:, n // 2, (n % 2) * 512:(n % 2 + 1) * 512], ps[:, 3 + n, :]).then_inc(sm["kvT_kept"], 1)

            def split(ch):
                ch.link(dve.tensor_copy(pieces[:, 0], q32_v))
                ch.link(dve.tensor_tensor(r_v, q32_v, pieces[:, 0], ALU.subtract))
                ch.link(dve.tensor_copy(pieces[:, 1], r_v))
                return dve.tensor_tensor(pieces[:, 2], r_v, pieces[:, 1], ALU.subtract)

            keep_kv(0)
            dve.wait_ge(sm["proj_kept"], 4)
            split(Chain(dve, sm["kv_sum"])).then_inc(sm["pieces_ready"], 1)
            keep_kv(4)
            dve.memset(kst[KR:KR + 32, :], 1.0).then_inc(sm["ones_set"], 1)

            dve.wait_ge(sm["pieces_stored"], 48)
            dve.wait_ge(sm["ohs"], 3)
            with dve.Fori(0, NTG) as g:
                b0 = 36 * g
                n = 0
                for q in range(2):
                    dve.wait_ge(sm["uT_ready"], 2 * g + q + 1)
                    dve.tensor_scalar(uT[:, q * 512:(q + 1) * 512], ps[0:R, q, :], srank[:, 0:1], None, ALU.mult
                                      ).then_inc(sm["uT_kept"], 1)
                dve.wait_ge(sm["emb_ready"], g + 1)
                emb = lambda j: ps[:, 2 + j // 2, (j % 2) * H:(j % 2 + 1) * H]
                stand(dve, "dve_go")
                for j in range(J):
                    dve.bn_stats(stats[:, j, :], emb(j)).then_inc(sm["prelude_chain"], 1)
                dve.wait_ge(sm["prelude_chain"], b0 + J)
                stand(dve, "dve_go")
                for j in range(J):
                    dve.bn_aggr(mv[:, j, :], stats[:, j, :]).then_inc(sm["prelude_chain"], 1)
                dve.wait_ge(sm["std_ready"], g + 1)
                dve.reciprocal(rstd[:, 0], std[:, :]).then_inc(sm["prelude_chain"], 1)
                dve.wait_ge(sm["prelude_chain"], b0 + 17)
                for j in range(J):
                    dve.tensor_scalar(y_v[:, j, :], emb(j), mv[:, j, 0:1], rstd[:, 0, j:j + 1], ALU.subtract, ALU.mult
                                      ).then_inc(sm["prelude_chain"], 1)
                dve.wait_ge(sm["prelude_chain"], b0 + 25)
                for j in range(J):
                    ins = dve.tensor_tensor(res[:, ds(g, 1), j * H:(j + 1) * H].rearrange("p o h -> p (o h)"),
                                            emb(j), y_v[:, j, :], ALU.add)
                    ins.then_inc(sm["prelude_chain"], 1)
                dve.wait_ge(sm["prelude_chain"], b0 + 33)
                dve.sem_inc(sm["y_ready"], 1)
                for k in range(KC):
                    for q in range(2):
                        dve.wait_ge(sm["yT_ready"], 4 * g + 2 * k + q + 1)
                        dst = yT_v[:, k].rearrange("p (t j) -> p j t", j=J)[:, 4 * q:4 * q + 4]
                        dve.tensor_copy(dst, ps[:, (6 + 2 * k + q) % 8, :].rearrange("p (j t) -> p j t", j=4)
                                        ).then_inc(sm["yT_kept"], 1)
                dve.wait_ge(sm["q_kept"], 4 * g + 4)
                dve.wait_ge(sm["q_pieces_stored"], 12 * 16 * g)
                dve.tensor_copy(pieces[:, 0], q32_v).then_inc(sm["prelude_chain"], 1)
                dve.wait_ge(sm["prelude_chain"], b0 + 34)
                dve.tensor_tensor(r_v, q32_v, pieces[:, 0], ALU.subtract).then_inc(sm["prelude_chain"], 1)
                dve.wait_ge(sm["prelude_chain"], b0 + 35)
                dve.tensor_copy(pieces[:, 1], r_v).then_inc(sm["prelude_chain"], 1)
                dve.wait_ge(sm["prelude_chain"], b0 + 36)
                dve.tensor_tensor(pieces[:, 2], r_v, pieces[:, 1], ALU.subtract).then_inc(sm["q_pieces_ready"], 1)

            def combine(m, u):
                if u == 0:
                    dve.wait_ge(sm["max_done"], 4 * TT * (m + 1))
                    dve.tensor_tensor(mxb[:, :], mx[:, ds(m % 2, 1), 0, :].rearrange("p o c -> p (o c)"),
                                      mx[:, ds(m % 2, 1), 1, :].rearrange("p o c -> p (o c)"), ALU.max
                                      ).then_inc(sm["max_chain"], 1)
                elif u == 1:
                    dve.wait_ge(sm["max_chain"], 2 * m + 1)
                    dve.tensor_scalar(mpc[:, 0:16], mxb[:, :], -1.0, None, ALU.mult).then_inc(sm["max_chain"], 1)
                elif u == 2:
                    dve.wait_ge(sm["max_chain"], 2 * m + 2)
                    dve.scalar_tensor_tensor(out=mpc[:, 16:32], in0=mxb[:, :], scalar=-1.0, in1=mpc[:, 0:16],
                                             op0=ALU.mult, op1=ALU.subtract).then_inc(sm["mpc_ready"], 1)
                else:
                    dve.wait_ge(sm["mpc_ready"], m + 1)
                    if not (isinstance(m, int) and m == 0):
                        dve.wait_ge(sm["m_loaded"], 128 * m)
                    dve.transpose(mrow[:, :], mpc[:, :]).then_inc(sm["mrow_ready"], 1)

            def block_dve(m, first=False, after=None):
                for t in range(TT):
                    for u in range(4):
                        j, half, st = 2 * (t % 2) + u // 2, u % 2, t // 2
                        dve.wait_ge(sm["max_ready"], 4 * (TT * m + t) + u + 1)
                        col = 4 * j + st
                        dve.tensor_reduce(mx[:, ds(m % 2, 1), half, col:col + 1].rearrange("p o c -> p (o c)"),
                                          ps[:, MAX_BANK + u, :], AX.X, ALU.max).then_inc(sm["max_done"], 1)
                        if t == 0 and not first:
                            combine(m - 1, u)
                    if after:
                        after(t)

            block_dve(0, first=True)
            block_dve(1)
            with dve.Fori(1, NBLK // 2 - 1) as u2:
                for par in range(2):
                    block_dve(2 * u2 + par)

            def invert0(t):
                if t == 1:
                    dve.wait_ge(sm["den_loaded"], 16)
                if 1 <= t <= 4:
                    dve.reciprocal(rden[0:64, (t - 1) * P:t * P], rden[0:64, (t - 1) * P:t * P]).then_inc(sm["t_chain"], 1)
                if t == 5:
                    dve.wait_ge(sm["t_chain"], 4)
                    dve.sem_inc(sm["rden_ready"], 1)

            block_dve(NBLK - 2, after=invert0)
            block_dve(NBLK - 1)
            for u in range(4):
                combine(NBLK - 1, u)

            def rsqrt_steps(link, rstd):
                link(dve.tensor_scalar(std[:, :], mv[:, :, 1], EPS, None, ALU.add))
                link(dve.tensor_scalar(ri[:, :], std[:, :].bitcast(I32), 1, None, ALU.arith_shift_right))
                link(dve.tensor_scalar(rstd.bitcast(I32), ri[:, :], -1.0, float(0x5f3759df), ALU.mult, ALU.add))
                for _ in range(4):
                    link(dve.tensor_tensor(rt[:, :], rstd, rstd, ALU.mult))
                    link(dve.tensor_tensor(rt[:, :], rt[:, :], std[:, :], ALU.mult))
                    link(dve.tensor_scalar(rt[:, :], rt[:, :], -0.5, 1.5, ALU.mult, ALU.add))
                    link(dve.tensor_tensor(rstd, rstd, rt[:, :], ALU.mult))

            n_chain = [4]

            def mark(ins):
                n_chain[0] += 1
                ins.then_inc(sm["t_chain"], 1)

            def settle():
                dve.wait_ge(sm["t_chain"], n_chain[0])

            def link(ins):
                mark(ins)
                settle()

            def residual(g):
                dve.wait_ge(sm[f"att_loaded{g}"], 16 * 16)
                dve.tensor_tensor(num[g % 2], num[g % 2], rdb[g % 2], ALU.mult).then_inc(sm["num_scaled"], 1)
                dve.wait_ge(sm["num_scaled"], g + 1)
                dve.tensor_tensor(pay[g][:, :, H:2 * H], res[:, g].rearrange("p (j h) -> p j h", j=J),
                                  num[g % 2].rearrange("p (j h) -> p j h", j=J), ALU.add).then_inc(sm["h2_ready"], 1)

            def statistics(g):
                hj = pay[g][:, :, H:2 * H]
                dve.wait_ge(sm["h2_ready"], g + 1)
                for j in range(J):
                    mark(dve.bn_stats(stats[:, j, :], hj[:, j]))
                settle()
                for j in range(J):
                    mark(dve.bn_aggr(mv[:, j, :], stats[:, j, :]))
                settle()
                rsqrt_steps(link, rstd[:, g % 2])

            def norm_dve(g):
                for j in range(J):
                    mark(dve.tensor_scalar(pay[g][:, j, 0:H], pay[g][:, j, H:2 * H], mv[:, j, 0:1], rstd[:, g % 2, j:j + 1],
                                           ALU.subtract, ALU.mult))
                settle()
                dve.sem_inc(sm["y2_ready"], 1)
                dve.sem_inc(sm["rstd_ready"], 1)

            def rstd_for_act(g):
                dve.scalar_tensor_tensor(out=nmr[:, g % 2], in0=mv[:, :, 0], scalar=-1.0, in1=rstd[:, g % 2],
                                         op0=ALU.mult, op1=ALU.mult).then_inc(sm["rstd_ready"], 1)
                dve.wait_ge(sm["rstd_ready"], g + 1)

            TURN_BANK = ((3, 4, 5, 6), (0, 1, 2, 4), (3, 5, 6, 7), (0, 1, 2, 4))

            def keep_y2_dve(g):
                dve.wait_ge(sm["num_scaled"], g + 1)
                for n in range(4):
                    dve.wait_ge(sm["tT_ready"], 4 * g + n + 1)
                    dve.tensor_copy(y2T[g][:, n // 2, (n % 2) * 512:(n % 2 + 1) * 512], ps[:, TURN_BANK[g][n], :]
                                    ).then_inc(sm["tT_kept"], 1)

            bj = lambda a: a[:, :].unsqueeze(2).broadcast_to([P, J, E])
            be_ = lambda a: a[:, :].unsqueeze(1).broadcast_to([P, J, E])

            def shift_logits(g):
                bank = TURN_BANK[g][0]
                dve.wait_ge(sm["lg_ready"], g + 1)
                lps = ps[:, bank, 0:J * E].rearrange("p (j e) -> p j e", j=J)
                link(dve.tensor_reduce(c1[:, :], lps, AX.X, ALU.max))
                dve.tensor_tensor(lg[:, :, :], lps, bj(c1), ALU.subtract).then_inc(sm["lg_shifted"], 1)

            def route(g):
                bank = TURN_BANK[g][0]
                dve.wait_ge(sm["ex_ready"], g + 1)
                link(dve.tensor_reduce(c2[:, :], ex[:, :, :], AX.X, ALU.add))
                link(dve.reciprocal(c3[:, :], c2[:, :]))
                link(dve.tensor_tensor(ex[:, :, :], ex[:, :, :], bj(c3), ALU.mult))
                link(dve.tensor_reduce(c1[:, :], ex[:, :, :], AX.X, ALU.max))
                link(dve.tensor_tensor(oh[:, :, :], ex[:, :, :], bj(c1), ALU.is_ge))
                link(dve.tensor_tensor(oh[:, :, :], oh[:, :, :], be_(rank8), ALU.mult))
                link(dve.tensor_reduce(c2[:, :], oh[:, :, :], AX.X, ALU.max))
                link(dve.tensor_tensor(oh[:, :, :], oh[:, :, :], bj(c2), ALU.is_equal))
                dve.tensor_reduce(cnt[:, :], oh[:, :, :].rearrange("p j e -> p e j"), AX.X, ALU.add).then_inc(sm["cnt_ready"], 1)
                link(dve.tensor_tensor(tmp[:, :, :], oh[:, :, :], be_(eid), ALU.mult))
                link(dve.tensor_reduce(c3[:, :], tmp[:, :, :], AX.X, ALU.add))
                dve.wait_ge(sm["pre_ready"], g + 1)
                link(dve.tensor_tensor(loc[:, 0, :], ps[:, bank, 64:64 + E], base[:, :], ALU.add))
                for j in range(1, J):
                    link(dve.tensor_tensor(loc[:, j, :], loc[:, j - 1, :], oh[:, j - 1, :], ALU.add))
                link(dve.tensor_tensor(base[:, :], ps[:, bank, 80:80 + E], base[:, :], ALU.add))
                link(dve.tensor_tensor(loc[:, :, :], loc[:, :, :], oh[:, :, :], ALU.mult))
                link(dve.tensor_reduce(c2[:, :], loc[:, :, :], AX.X, ALU.add))
                link(dve.tensor_scalar(kept[:, :], c2[:, :], float(CAP), None, ALU.is_lt))
                mark(dve.tensor_tensor(pay[g][:, :, 2 * H], c1[:, :], kept[:, :], ALU.mult))
                mark(dve.tensor_copy(pay[g][:, :, 2 * H + 1], tid[:, :]))
                link(dve.scalar_tensor_tensor(out=slot[:, :], in0=c3[:, :], scalar=float(CAP), in1=c2[:, :],
                                              op0=ALU.mult, op1=ALU.add))
                link(dve.tensor_scalar(c2[:, :], kept[:, :], float(-2 * E * CAP), float(2 * E * CAP), ALU.mult, ALU.add))
                dve.tensor_tensor(sidx[:, g], slot[:, :], c2[:, :], ALU.add).then_inc(sm["sidx_ready"], 1)
                link(dve.tensor_scalar(tid[:, :], tid[:, :], float(TG), None, ALU.add))

            statistics(0)
            norm_dve(0)
            statistics(1)
            keep_y2_dve(0)
            norm_dve(1)
            shift_logits(0)
            route(0)
            dve.wait_ge(sm["den_loaded"], 32)
            dve.reciprocal(rden[64:P], rden[64:P]).then_inc(sm["rden_ready"], 1)
            shift_logits(1)
            route(1)
            residual(2)
            statistics(2)
            rstd_for_act(2)
            residual(3)
            statistics(3)
            rstd_for_act(3)
            shift_logits(2)
            route(2)
            shift_logits(3)
            route(3)

            dve.wait_ge(sm["scattered"], 16 * NTG * J)
            dve.sem_inc(sm["y_free0"], 1)
            dve.sem_inc(sm["y_free1"], 1)
            with dve.Fori(0, E // 4) as u:
                for par in range(4):
                    e, half = 4 * u + par, par % 2
                    dve.wait_ge(sm[f"x_loaded{par}"], 32 * u + 32)
                    dve.wait_ge(sm[f"out_stored{par}"], 64 * u)
                    tok = x_load[par][:, :, 2 * H + 1]
                    dve.tensor_scalar(empty[:, par], tok, 0.0, float(2 * B * S), ALU.is_equal, ALU.mult).then_inc(sm["e_chain"], 1)
                    dve.wait_ge(sm["e_chain"], 4 * e + 1)
                    dve.scalar_tensor_tensor(out=oidx[:, par], in0=tok, scalar=-1.0, in1=empty[:, par],
                                             op0=ALU.add, op1=ALU.add).then_inc(sm["e_chain"], 1)
                    for n in range(2):
                        dve.wait_ge(sm[f"e_ready{half}"], 2 * (2 * u + par // 2) + n + 1)
                        dve.tensor_tensor(y_sum[:, half, 2 * n:2 * n + 2],
                                          ps[:, 4 + 2 * half + n].rearrange("p (n h) -> p n h", n=2),
                                          bb[:, par].unsqueeze(1).broadcast_to([P, 2, H]), ALU.add).then_inc(sm["e_chain"], 1)
                    dve.wait_ge(sm["e_chain"], 4 * e + 4)
                    dve.sem_inc(sm[f"y_free{half}"], 1)
                    for n in range(4):
                        dve.scalar_tensor_tensor(out=y_out[:, par, n], in0=y_sum[:, half, n],
                                                 scalar=x_load[par][:, n, 2 * H:2 * H + 1],
                                                 in1=x_load[par][:, n, H:2 * H], op0=ALU.mult, op1=ALU.add
                                                 ).then_inc(sm["y_chain"], 1)
                    dve.wait_ge(sm["y_chain"], 4 * e + 4)
                    dve.sem_inc(sm["y_out_ready"], 1)


_INS = ['x', 'L0_tok_U', 'L0_tok_s', 'L0_tok_Vt', 'L0_attn_keys', 'L0_attn_values', 'L0_attn_Wq_w', 'L0_attn_Wq_b',
        'L0_attn_Wk_w', 'L0_attn_Wk_b', 'L0_attn_Wv_w', 'L0_attn_Wv_b', 'L0_ffn_wg', 'L0_ffn_W', 'L0_ffn_b']


def kernel(**inputs):
    import numpy as _np
    import concourse.bacc as _bacc
    from concourse import mybir as _mybir
    from concourse.bass_utils import run_bass_kernel_spmd as _run

    nc = _bacc.Bacc("TRN2", target_bir_lowering=False, num_devices=1)
    arrays, args = {}, []
    for name in _INS:
        a = _np.ascontiguousarray(inputs[name])
        arrays[f"in_{name}"] = a
        args.append(nc.dram_tensor(f"in_{name}", a.shape, _mybir.dt.from_np(a.dtype), kind="ExternalInput").ap())
    args.append(nc.dram_tensor("out_h", (B * S, H), _mybir.dt.float32, kind="ExternalOutput").ap())
    build(nc, *args)
    r = _run(nc, [arrays], core_ids=[0])
    return r.results[0]["out_h"].reshape(B, S, H)
```

```python
from contextlib import ExitStack

import concourse.bass as bass
import numpy as np
from concourse import mybir
from concourse.bass import ds

ALU = mybir.AluOpType
ACT = mybir.ActivationFunctionType
AX = mybir.AxisListType
F32 = mybir.dt.float32
BF16 = mybir.dt.bfloat16
I32 = mybir.dt.int32

P = 128
V, R = 25000, 64
H = 256
KC = H // P
B, S, T = 2, 2048, 1024
NH = 16
DH = H // NH
HG = 4
NG = NH // HG
SB = 512
NSB = S // SB
NBLK = B * NG * NSB
TT = T // P
J = 8
TG = P * J
NTG = B * S // TG
E = 8
CAP = B * S // E
EPS = 1e-5
SCALE = float(DH) ** -0.5
PIECES = (0, 0, 0, 1, 1, 2)
KPIECES = (0, 1, 2, 0, 1, 0)
KR = 16 * len(PIECES)
AHEAD = 13
PAY = 2 * H + 2
LAST = NBLK * TT
RING = 4


ONE_ONE = float(np.array([0x3F803F80], np.uint32).view(np.float32)[0])


class Chain:

    def __init__(self, eng, sem):
        self.eng, self.sem, self.n = eng, sem, 0

    def mark(self, ins):
        ins.then_inc(self.sem, 1)
        self.n += 1
        return self.n

    def link(self, ins):
        self.mark(ins)
        self.eng.wait_ge(self.sem, self.n)


def build(nc, x, U, s_rank, Vt, keys, values, Wq_w, Wq_b, Wk_w, Wk_b, Wv_w, Wv_b, wg, We, be, out):
    with ExitStack() as ctx:
        def sb(name, shape, dt=F32):
            return ctx.enter_context(nc.sbuf_tensor(name, shape, dt))

        def sem(name):
            return ctx.enter_context(nc.semaphore(name))

        q_dram = nc.dram_tensor("q_dram", (3, NBLK, HG * DH, SB), BF16).ap()
        k_dram = nc.dram_tensor("k_dram", (3, H, T), BF16).ap()
        a_dram = nc.dram_tensor("a_dram", (NBLK, P, SB), F32).ap()
        xd_dram = nc.dram_tensor("xd_dram", (E * CAP, PAY), F32).ap()
        rd_dram = nc.dram_tensor("rd_dram", (NBLK, HG, SB), F32).ap()

        res_area = sb("res_area", [P, NTG * J * H + 2 * J])
        res = [res_area[:, g * J * H + g // 2 * 2 * J:(g + 1) * J * H + g // 2 * 2 * J] for g in range(NTG)]
        kst = sb("kst", [P, NH * T], BF16)
        qst = sb("qst", [P, 4, HG, SB], BF16)
        vaug = sb("vaug", [P, NG, TT * HG * 32])
        vblk = sb("vblk", [P, TT, HG, 32])
        probs_area = sb("probs_area", [P, 2 * J * PAY])
        probs = probs_area[:, 0:4 * RING * SB].rearrange("p (r s) -> p r s", s=2 * SB)
        acc = sb("acc", [P, 2, SB])
        ident = sb("ident", [P, P])
        identb = sb("identb", [P, P], BF16)
        upper = sb("upper", [P, P])
        ones = sb("ones", [P, P])
        mx = sb("mx", [P, 2, 16])
        mpc = sb("mpc", [P, 32], BF16)
        mrow = sb("mrow", [P, 32], BF16)
        idx = sb("idx", [P, NTG * J], I32)
        srank = sb("srank", [R, 1])
        vt = sb("vt", [R, H])
        bq = sb("bq", [P, KC])
        bk = sb("bk", [P, KC])
        bv = sb("bv", [1, H])
        wgs = sb("wgs", [P, KC, E])
        early = sb("early", [P, 7680])
        wload = early[:, 0:1536].rearrange("p (w c h) -> p w c h", w=3, c=KC)
        wT = early[:, 1536:3072].rearrange("p (w c h) -> p w c h", w=3, c=KC)
        uT = early[0:R, 3072:4096]
        stats = sb("stats", [P, J, 6])
        mv = sb("mv", [P, J, 2])
        std = sb("std", [P, J])
        ri = sb("ri", [P, J], I32)
        rt = sb("rt", [P, J])
        rstd = sb("rstd", [P, 2, J])
        eidi = sb("eidi", [P, E], I32)
        eid = sb("eid", [P, E])
        rank8 = sb("rank8", [P, E])
        tidi = sb("tidi", [P, J], I32)
        tid = sb("tid", [P, J])
        lg = sb("lg", [P, J, E])
        ex = sb("ex", [P, J, E])
        oh = sb("oh", [P, J, E])
        loc = sb("loc", [P, J, E])
        tmp = sb("tmp", [P, J, E])
        c1 = sb("c1", [P, J])
        c2 = sb("c2", [P, J])
        c3 = sb("c3", [P, J])
        slot = sb("slot", [P, J])
        kept = sb("kept", [P, J])
        cnt = sb("cnt", [P, E])
        base = sb("base", [P, E])
        sidx = sb("sidx", [P, NTG, J], I32)
        pay_area = sb("pay_area", [P, 2 * J * PAY])
        oidx = sb("oidx", [P, 4, HG], I32)
        empty = sb("empty", [P, 4, HG])
        nmr = sb("nmr", [P, 2, J])

        def view(k):
            return probs[:, 2 * k:2 * k + 2, :].rearrange("p a b -> p (a b)")
        y_v = view(0).rearrange("p (j h) -> p j h", j=J)
        yT_v = view(1).rearrange("p (k t) -> p k t", k=KC)
        wide_a = view(2).rearrange("p (k t) -> p k t", k=KC)
        wide_b = view(3).rearrange("p (k t) -> p k t", k=KC)
        kst32 = kst[:, :].bitcast(F32)
        pays = [a[:, n * J * PAY:(n + 1) * J * PAY].rearrange("p (j h) -> p j h", j=J)
                for a in (pay_area, probs_area, res_area) for n in range(2) if (n + 1) * J * PAY <= a.shape[1]]
        pay = [pays[0], pays[1], pays[4], pays[3]]
        x_load = [p[:, 0:HG] for p in pays[0:4]]
        ZERO_PARTS = 16
        zeros = pay_area[:, 0:E * CAP // ZERO_PARTS // P * PAY]
        gemb = pay_area[:, HG * PAY:HG * PAY + NTG * J * R].rearrange("p (g j r) -> p g j r", g=NTG, j=J)
        keys_in = y_v
        q32 = [wide_a, wide_b]
        pieces = [early[:, 4608:7680], pay_area[:, 2 * HG * PAY:2 * HG * PAY + 3072]]
        pieces = [a.bitcast(BF16).rearrange("p (r c t) -> p r c t", r=3, c=KC) for a in pieces]
        KEYS, VALUES = 0, NTG + 1
        ORDER = [(a, KEYS, m) for a in "tp" for m in range(4)] + [("t", VALUES, m) for m in range(4)]
        for g in range(NTG):
            ORDER += [(a, g + 1, m) for a in "tp" for m in range(4)] + [("p", VALUES, g)]
        CHUNK = {c: n for n, c in enumerate(ORDER)}
        RDEN_BLOCKS = ((0, 24), (24, NBLK))
        SLOT = (0, 1, 0, 1, 0)
        qst32 = qst[:, :, :, :].rearrange("p a j s -> p (a j s)").bitcast(F32)
        values_in = qst32[:, 0:2048].rearrange("p (j h) -> p j h", j=J)
        vT = qst32[:, 2048:4096].rearrange("p (k t) -> p k t", k=KC)
        num = [early[:, 0:2048], early[:, 2048:4096]]
        rden = early[:, 4096:4608]
        rdb = [early[:, 4608:6656], vaug[:, 0:2].rearrange("p a b -> p (a b)")]
        y2T = [a.rearrange("p (k t) -> p k t", k=KC) for a in
               [rdb[1]] + 3 * [vaug[:, 2:4].rearrange("p a b -> p (a b)")]]
        xe_T = [vaug[:, 2 + n].rearrange("p (c t) -> p c t", c=KC) for n in range(2)]
        we_load = kst32[:, 0:4096].rearrange("p (e c h) -> p e c h", e=E, c=KC)
        we_T = kst32[:, 4096:8192].rearrange("p (e n) -> p e n", e=E)
        flat = res_area
        y_out = flat[:, 0:4096].rearrange("p (e n h) -> p e n h", e=4, n=HG)
        y_sum = flat[:, 4096:6144].rearrange("p (e n h) -> p e n h", e=2, n=HG)
        bb = flat[:, 6144:7168].rearrange("p (e h) -> p e h", e=4)
        we_now = flat[:, 7168:8192].rearrange("p (e n) -> p e n", e=2)

        ps = ctx.enter_context(nc.psum_tensor("ps", [P, 8, 512], F32))
        MAX_BANK, PV_BANK = 3, 7
        EXP_BANK = (0, 1, 2, 1)
        EXP_BACK = (4, 2, 4, 2)

        names = """w_loaded c_loaded s_loaded keys_loaded values_loaded idx_loaded const_made wT_ready wT_kept
            rows_gathered0 rows_gathered1 rows_gathered2 rows_gathered3 uT_ready uT_kept emb_ready
            prelude_rstd y_ready res_made chunk_ready chunk_kept split_done pieces_stored
            k_stacked ones_set ones_row_set ones_made prelude_chain q_stored0 q_stored1 q_stored2 q_stored3
            q_loaded va_loaded vb_loaded scores_ready exp_done pv_done max_ready max_done max_chain
            mpc_ready mrow_ready m_loaded acc_ready acc_stored
            zeroed att_loaded0 att_loaded1 att_loaded2 att_loaded3 tail_chain y2_ready tT_ready tT_kept lg_ready
            lg_shifted ex_ready count_ready prefix_ready sidx_ready scattered x_loaded0 x_loaded1 x_loaded2 x_loaded3
            xT_ready xT_kept e_ready0 e_ready1 y_free0 y_free1 e_chain y_chain y_out_ready we_kept
            out_stored0 out_stored1 out_stored2 out_stored3 base_stored den_loaded we_loaded rden_ready rden_stored
            h2_ready num_scaled weT_ready weT_kept rstd_ready zeros_set const_chain pool_go""".split()
        sm = {n: sem(n) for n in names}

        def stand(eng, name):
            eng.sem_inc(sm[name], 1)

        block = ctx.enter_context(nc.Block())

        @block.sync
        def _(sp):
            sp.dma_start(idx[:, :].rearrange("p (b h j) -> p b h j", b=B, j=J),
                         x.rearrange("b (h p j) -> p b h j", p=P, j=J)).then_inc(sm["idx_loaded"], 16)
            for n, w in ((1, Wk_w), (0, Wq_w), (2, Wv_w)):
                sp.dma_start(wload[:, n], w.rearrange("(c p) h -> p c h", p=P)).then_inc(sm["w_loaded"], 16)
            sp.dma_start(srank[:, :], s_rank.rearrange("(r o) -> r o", o=1), allow_slow_non_contiguous=True).then_inc(sm["s_loaded"], 16)
            sp.dma_start(vt[:, :], Vt).then_inc(sm["s_loaded"], 16)
            sp.dma_start(keys_in, keys.rearrange("o (n p) h -> p (o n) h", p=P)).then_inc(sm["keys_loaded"], 16)
            sp.dma_start(bq[:, :], Wq_b.rearrange("(c p) -> p c", p=P), allow_slow_non_contiguous=True).then_inc(sm["c_loaded"], 16)
            sp.dma_start(bk[:, :], Wk_b.rearrange("(c p) -> p c", p=P), allow_slow_non_contiguous=True).then_inc(sm["c_loaded"], 16)
            sp.dma_start(bv[:, :], Wv_b.rearrange("(o h) -> o h", o=1)).then_inc(sm["c_loaded"], 16)
            sp.dma_start(wgs[:, :, :], wg.rearrange("(c p) e -> p c e", p=P)).then_inc(sm["c_loaded"], 16)
            sp.dma_start(values_in, values.rearrange("o (n p) h -> p (o n) h", p=P)).then_inc(sm["values_loaded"], 16)
            sp.wait_ge(sm["split_done"], 1)
            for r in range(3):
                sp.dma_start(k_dram[r].rearrange("(c p) t -> p c t", p=P), pieces[0][:, r]).then_inc(sm["pieces_stored"], 16)
            sp.wait_ge(sm["pieces_stored"], 48)
            for r, pc in enumerate(KPIECES):
                sp.dma_start(kst[16 * r:16 * r + 16, :].rearrange("p (h t) -> p h t", h=NH),
                             k_dram[pc].rearrange("(h i) t -> i h t", i=DH)).then_inc(sm["k_stacked"], 16)

            def store_q(g):
                sp.wait_ge(sm["split_done"], g + 2)
                for r in range(3):
                    for c in range(KC):
                        for hh in range(2):
                            n0 = (g // 2) * 16 + (g % 2) * 2 + (2 * c + hh) * 4
                            sp.dma_start(q_dram[r, n0:n0 + 2].rearrange("n p s -> p n s"),
                                         pieces[SLOT[g + 1]][64 * hh:64 * hh + 64, r, c].rearrange("p (n s) -> p n s", n=2)
                                         ).then_inc(sm[f"q_stored{g}"], 16)

            def load_q(i):
                for r, pc in enumerate(PIECES):
                    sp.dma_start(qst[16 * r:16 * r + 16, ds(i % 4, 1)].rearrange("p o j s -> p (o j) s"),
                                 q_dram[pc, ds(i, 1)].rearrange("o (j i) s -> (o i) j s", i=DH)
                                 ).then_inc(sm["q_loaded"], 16)

            def load_v(i, half):
                n = HALF_V
                sp.dma_start(vblk[:, 4 * half:4 * half + 4].rearrange("p t j c -> p (t j c)"),
                             vaug[:, ds((i // NSB) % NG, 1), half * n:(half + 1) * n].rearrange("p o n -> p (o n)")
                             ).then_inc(sm["vb_loaded" if half else "va_loaded"], 16)

            def load_m(i):
                sp.wait_ge(sm["mrow_ready"], i + 1)
                for c in range(2):
                    row = qst[KR + c:KR + c + 1, ds(i % 4, 1)].rearrange("p o j (t q s) -> p (o j t) q s", q=4, s=32)
                    for q in range(4):
                        sp.dma_start(row[:, :, q, :], mrow[32 * q + 16 * c:32 * q + 16 * c + 16, :]
                                     ).then_inc(sm["m_loaded"], 16)

            HALF_V = 4 * HG * 32
            store_q(0)
            store_q(1)
            for g in range(2):
                sp.wait_ge(sm[f"q_stored{g}"], 12 * 16)
            for i in range(3):
                if i == 2:
                    sp.wait_ge(sm["chunk_kept"], len(ORDER))
                load_q(i)
                if i < 2:
                    sp.wait_ge(sm["q_loaded"], 96 * (i + 1))
            store_q(2)
            store_q(3)
            sp.wait_ge(sm["ones_row_set"], 1)
            load_v(0, 0)
            for g in range(2, NTG):
                sp.wait_ge(sm[f"q_stored{g}"], 12 * 16)
            load_m(0)

            def store_acc(i):
                sp.wait_ge(sm["acc_ready"], i + 1)
                sp.dma_start(a_dram[ds(i, 1)].rearrange("o p s -> (o p) s"),
                             acc[:, ds(i % 2, 1)].rearrange("p o s -> p (o s)")).then_inc(sm["acc_stored"], 16)

            def block_sp(i, first=False, more_q=True, more=True, mid=None, end=None):
                sp.wait_ge(sm["pv_done"], TT * i)
                load_v(i, 1)
                if not first:
                    store_acc(i - 1)
                if more_q:
                    sp.wait_ge(sm["scores_ready"], HG * TT * i)
                    sp.wait_ge(sm["q_loaded"], 96 * (i + 3))
                    load_q(i + 3)
                if more:
                    load_m(i + 1)
                    if mid:
                        mid()
                    sp.wait_ge(sm["pv_done"], TT * i + 4)
                    load_v(i + 1, 0)
                if end:
                    end()

            block_sp(0, first=True)
            with sp.Fori(0, (NBLK - 6) // 2) as u:
                for par in range(2):
                    block_sp(2 * u + par + 1)

            def load_den(lo, hi):
                sp.wait_ge(sm["acc_stored"], 16 * hi)
                sp.dma_start(rden[HG * lo:HG * hi], a_dram[lo:hi].rearrange("n (j y) s -> (n j) y s", j=HG)[:, DH]
                             ).then_inc(sm["den_loaded"], 16)

            def store_rden(part):
                lo, hi = RDEN_BLOCKS[part]
                sp.wait_ge(sm["rden_ready"], part + 1)
                sp.dma_start(rd_dram[lo:hi].rearrange("n j s -> (n j) s"), rden[HG * lo:HG * hi]
                             ).then_inc(sm["rden_stored"], 16)

            def load_num(g):
                for q in range(2):
                    for j in range(HG):
                        p0 = 64 * q + DH * j
                        n0 = 8 * g + 4 * q
                        sp.dma_start(num[g % 2][p0:p0 + DH].rearrange("p (n s) -> p n s", n=4),
                                     a_dram[n0:n0 + 4, 32 * j:32 * j + DH].rearrange("n x s -> x n s")
                                     ).then_inc(sm[f"att_loaded{g}"], 16)

            def load_rdb(g):
                sp.wait_ge(sm["rden_stored"], 32 if g == NTG - 1 else 16)
                for q in range(2):
                    for j in range(HG):
                        p0 = 64 * q + DH * j
                        n0 = 8 * g + 4 * q
                        sp.dma_start(rdb[g % 2][p0:p0 + DH].rearrange("p (n s) -> p n s", n=4),
                                     rd_dram[n0:n0 + 4, j].unsqueeze(0).broadcast_to([DH, 4, SB])
                                     ).then_inc(sm[f"att_loaded{g}"], 16)

            def store_base(g):
                sp.wait_ge(sm["h2_ready"], g + 1)
                sp.dma_start(out[g * TG:(g + 1) * TG].rearrange("(p j) h -> p j h", p=P), pay[g][:, :, H:2 * H]
                             ).then_inc(sm["base_stored"], 16)

            def nums():
                load_num(0)
                load_num(1)

            def rdb0():
                store_rden(0)
                load_rdb(0)

            def rdb1():
                sp.wait_ge(sm["vb_loaded"], 16 * (NBLK - 2))
                load_rdb(1)

            def att2():
                sp.wait_ge(sm["h2_ready"], 1)
                load_num(2)
                load_rdb(2)

            def bases():
                load_den(24, NBLK - 1)
                store_base(0)
                store_base(1)

            block_sp(NBLK - 5, end=lambda: load_den(0, 24))
            block_sp(NBLK - 4, end=nums)
            block_sp(NBLK - 3, more_q=False, end=rdb0)
            block_sp(NBLK - 2, more_q=False, mid=rdb1, end=att2)
            block_sp(NBLK - 1, more_q=False, more=False, end=bases)
            sp.wait_ge(sm["acc_ready"], NBLK)
            sp.dma_start(rden[P - HG:P], acc[DH:P:32, (NBLK - 1) % 2]).then_inc(sm["den_loaded"], 16)
            store_acc(NBLK - 1)
            sp.wait_ge(sm["acc_stored"], 16 * NBLK)
            sp.wait_ge(sm["pv_done"], TT * NBLK)
            sp.wait_ge(sm["h2_ready"], 2)
            load_num(3)
            store_rden(1)
            sp.wait_ge(sm["lg_ready"], 1)
            load_rdb(3)
            sp.dma_start(we_load, We.rearrange("e (c p) h -> p e c h", p=P)).then_inc(sm["we_loaded"], 16)
            store_base(2)
            store_base(3)

            sp.wait_ge(sm["scattered"], NTG * J * 16)

            def load_expert(e, par):
                sp.dma_start(x_load[par], xd_dram[ds(e * CAP, CAP)].rearrange("(n p) h -> p n h", p=P)
                             ).then_inc(sm[f"x_loaded{par}"], 16)
                sp.dma_start(bb[:, par], be[ds(e, 1)].broadcast_to([P, H])).then_inc(sm[f"x_loaded{par}"], 16)

            sp.wait_ge(sm["base_stored"], NTG * 16)
            for par in range(4):
                load_expert(par, par)
            for par in range(4):
                sp.wait_ge(sm[f"out_stored{par}"], 16 * HG)
                load_expert(par + 4, par)

        @block.gpsimd
        def _(pool):
            ch = Chain(pool, sm["const_chain"])
            ch.link(pool.memset(ident[:, :], 0.0))
            ch.link(pool.memset(upper[:, :], 1.0))
            ch.link(pool.affine_select(out=ident[:, :], in_=ident[:, :], compare_op=ALU.not_equal, fill=1.0,
                                       base=0, pattern=[[-1, P]], channel_multiplier=1))
            ch.link(pool.affine_select(out=upper[:, :], in_=upper[:, :], compare_op=ALU.is_gt, fill=0.0,
                                       base=0, pattern=[[1, P]], channel_multiplier=-1))
            ch.link(pool.iota(eidi[:, :], [[1, E]], 0, 0))
            ch.link(pool.iota(tidi[:, :], [[1, J]], 1, J))
            ch.link(pool.tensor_copy(identb[:, :], ident[:, :]))
            ch.link(pool.tensor_copy(eid[:, :], eidi[:, :]))
            ch.link(pool.tensor_copy(tid[:, :], tidi[:, :]))
            pool.tensor_scalar(rank8[:, :], eid[:, :], -1.0, float(E), ALU.mult, ALU.add).then_inc(sm["const_made"], 1)
            pool.wait_ge(sm["idx_loaded"], 16)
            for g in range(NTG):
                for j in range(J):
                    pool.indirect_dma_start(gemb[:, g, j], None, U, bass.IndirectOffsetOnAxis(ap=idx[:, g * J + j:g * J + j + 1], axis=0)
                                            ).then_inc(sm[f"rows_gathered{g}"], 16)
            pool.wait_ge(sm["const_made"], 1)
            pool.memset(kst32[KR:KR + 32, :], ONE_ONE).then_inc(sm["ones_row_set"], 1)
            pool.wait_ge(sm["zeros_set"], 1)
            with pool.Fori(0, ZERO_PARTS) as n:
                pool.wait_ge(sm["mrow_ready"], n + 1)
                stand(pool, "pool_go")
                pool.dma_start(xd_dram[ds(n * (E * CAP // ZERO_PARTS), E * CAP // ZERO_PARTS), :]
                               .rearrange("(p j) h -> p (j h)", p=P), zeros).then_inc(sm["zeroed"], 16)
            pool.wait_ge(sm["zeroed"], 16 * ZERO_PARTS)
            for g in range(NTG - 1):
                pool.wait_ge(sm[f"att_loaded{g}"], 16 * 16)
                if g:
                    pool.wait_ge(sm["h2_ready"], g)
                pool.tensor_tensor(num[g % 2], num[g % 2], rdb[g % 2], ALU.mult).then_inc(sm["num_scaled"], 1)
                pool.wait_ge(sm["num_scaled"], g + 1)
                pool.tensor_tensor(pay[g][:, :, H:2 * H], res[g].rearrange("p (j h) -> p j h", j=J),
                                   num[g % 2].rearrange("p (j h) -> p j h", j=J), ALU.add).then_inc(sm["h2_ready"], 1)
            pool.wait_ge(sm["zeroed"], 16 * ZERO_PARTS)
            for g in range(NTG):
                pool.wait_ge(sm["sidx_ready"], g + 1)
                for j in range(J):
                    pool.indirect_dma_start(
                        xd_dram, bass.IndirectOffsetOnAxis(ap=sidx[:, g, j:j + 1], axis=0), pay[g][:, j], None,
                        bounds_check=E * CAP - 1, oob_is_err=False).then_inc(sm["scattered"], 16)
            pool.wait_ge(sm["base_stored"], 16 * NTG)
            with pool.Fori(0, E // 4) as u:
                for par in range(4):
                    pool.wait_ge(sm["y_out_ready"], 4 * u + par + 1)
                    stand(pool, "pool_go")
                    for n in range(4):
                        pool.indirect_dma_start(
                            out, bass.IndirectOffsetOnAxis(ap=oidx[:, par, n:n + 1], axis=0), y_out[:, par, n], None,
                            bounds_check=B * S - 1, oob_is_err=False).then_inc(sm[f"out_stored{par}"], 16)
            for par in range(4):
                pool.wait_ge(sm[f"out_stored{par}"], 16 * E)

        @block.tensor
        def _(pe):
            pe.wait_ge(sm["w_loaded"], 48)
            pe.wait_ge(sm["const_made"], 1)
            for n, w in enumerate((1, 0, 2)):
                for k in range(KC):
                    for c in range(KC):
                        mm = pe.transpose(ps[:, n, (k * KC + c) * P:(k * KC + c + 1) * P],
                                          wload[:, w, c, k * P:(k + 1) * P], ident[:, :])
                mm.then_inc(sm["wT_ready"], 1)

            def turn_rows(st, src):
                for m in range(4):
                    n = CHUNK["t", st, m]
                    k, q = m // 2, m % 2
                    if n >= 2:
                        pe.wait_ge(sm["chunk_kept"], n - 1)
                    for r in range(4):
                        mm = pe.transpose(ps[:, 6 + n % 2, r * P:(r + 1) * P], src[:, 4 * q + r, k * P:(k + 1) * P], ident[:, :])
                    mm.then_inc(sm["chunk_ready"], 1)

            def project(st, w):
                pe.wait_ge(sm["chunk_kept"], CHUNK["t", st, 3] + 1)
                for m in range(4):
                    n = CHUNK["p", st, m]
                    pe.wait_ge(sm["chunk_kept"], n - 1)
                    c, half = m // 2, m % 2
                    for k in range(KC):
                        mm = pe.matmul(ps[:, 6 + n % 2, :], wT[:, w, k, c * P:(c + 1) * P],
                                       yT_v[:, k, half * 512:(half + 1) * 512], start=(k == 0), stop=(k == 1))
                    mm.then_inc(sm["chunk_ready"], 1)

            def project_v(m):
                n = CHUNK["p", VALUES, m]
                pe.wait_ge(sm["chunk_kept"], n - 1)
                for u in range(2):
                    t0, o = (2 * m + u) * P, ps[:, 6 + n % 2, u * H:(u + 1) * H]
                    for k in range(KC):
                        pe.matmul(o, vT[:, k, t0:t0 + P], wT[:, 2, k, :], start=(k == 0), stop=False)
                    mm = pe.matmul(o, ones[0:1, :], bv[:, :], start=False, stop=True)
                mm.then_inc(sm["chunk_ready"], 1)

            def embed(g):
                pe.wait_ge(sm[f"rows_gathered{g}"], 16 * J)
                if g == 0:
                    pe.wait_ge(sm["wT_kept"], 3)
                for q in range(2):
                    for n in range(4):
                        mm = pe.transpose(ps[0:R, q, n * P:(n + 1) * P], gemb[:, g, 4 * q + n, :], ident[:, :])
                    mm.then_inc(sm["uT_ready"], 1)
                pe.wait_ge(sm["uT_kept"], 2 * g + 2)
                if g:
                    pe.wait_ge(sm["res_made"], g)
                for j in range(J):
                    mm = pe.matmul(ps[:, 2 + j // 2, (j % 2) * H:(j % 2 + 1) * H], uT[:, j * P:(j + 1) * P], vt[:, :],
                                   start=True, stop=True)
                mm.then_inc(sm["emb_ready"], 1)

            def token_group(g):
                pe.wait_ge(sm["y_ready"], g + 1)
                turn_rows(g + 1, y_v)
                project(g + 1, 0)
                project_v(g)

            pe.wait_ge(sm["s_loaded"], 32)
            embed(0)
            pe.wait_ge(sm["keys_loaded"], 16)
            turn_rows(0, keys_in)
            project(0, 1)
            pe.wait_ge(sm["values_loaded"], 16)
            turn_rows(VALUES, values_in)
            pe.wait_ge(sm["c_loaded"], 4 * 16)
            pe.wait_ge(sm["ones_made"], 1)
            for g in range(1, NTG):
                embed(g)
                token_group(g - 1)
            token_group(NTG - 1)

            pe.wait_ge(sm["k_stacked"], 6 * 16)
            pe.wait_ge(sm["ones_row_set"], 1)
            pe.wait_ge(sm["res_made"], NTG)
            pe.wait_ge(sm["chunk_kept"], len(ORDER))
            pe.wait_ge(sm["const_made"], 1)

            def maximum(m, t, gi, u):
                if t == 0 and u == 0:
                    pe.wait_ge(sm["q_loaded"], 96 * (m + 1))
                hg = (m // NSB) % NG
                j, half, st = 2 * (t % 2) + u // 2, u % 2, t // 2
                if u % 2 == 0 and not (isinstance(gi, int) and gi == 0):
                    pe.wait_ge(sm["max_done"], 2 * gi + u // 2 - 1)
                mm = pe.matmul(ps[:, MAX_BANK + u, :],
                          qst[0:KR, ds(m % 4, 1), j, st * P:(st + 1) * P].rearrange("p o s -> p (o s)"),
                          kst[0:KR, ds((hg * HG + j) * T + half * 512, 512)],
                          start=True, stop=True)
                if u % 2:
                    mm.then_inc(sm["max_ready"], 1)

            def score(i, t, j):
                hg = (i // NSB) % NG
                n = HG * TT * i + HG * t + j + 1 - EXP_BACK[j]
                if not (isinstance(n, int) and n < 1):
                    pe.wait_ge(sm["exp_done"], n)
                pe.matmul(ps[:, EXP_BANK[j], :], kst[0:KR + 2, ds((hg * HG + j) * T + t * P, P)],
                          qst[0:KR + 2, ds(i % 4, 1), j, :].rearrange("p o s -> p (o s)"),
                          start=True, stop=True).then_inc(sm["scores_ready"], 1)

            def pv(i, t):
                pe.wait_ge(sm["exp_done"], HG * (TT * i + t + 1))
                if t == 0:
                    pe.wait_ge(sm["va_loaded"], 16 * (i + 1))
                    pe.wait_ge(sm["acc_ready"], i)
                if t == 4:
                    pe.wait_ge(sm["vb_loaded"], 16 * (i + 1))
                for j in range(HG):
                    mm = pe.matmul(ps[32 * j:32 * j + 32, PV_BANK, :], vblk[:, t, j, :],
                                   probs[:, 2 * (t % RING) + j // 2, (j % 2) * SB:(j % 2 + 1) * SB],
                                   start=(t == 0), stop=(t == TT - 1))
                mm.then_inc(sm["pv_done"], 1)

            def block_pe(i, first=False, ahead=TT, extra={}):
                pe.wait_ge(sm["m_loaded"], 128 * (i + 1))
                for t in range(TT):
                    far = t + AHEAD
                    if t in extra:
                        extra[t]()
                    for step in "s0 m0 s1 s2 m1 pv s3 m2 m3".split():
                        if step[0] == "s":
                            score(i, t, int(step[1]))
                        elif step == "pv":
                            if t:
                                pv(i, t - 1)
                            elif not first:
                                pv(i - 1, TT - 1)
                        elif t < ahead:
                            maximum(i + far // TT, far % TT, TT * i + far, int(step[1]))

            for gi in range(AHEAD):
                for u in range(4):
                    maximum(gi // TT, gi % TT, gi, u)
            block_pe(0, first=True)
            with pe.Fori(0, (NBLK - 4) // 2) as u:
                for par in range(2):
                    block_pe(2 * u + par + 1)
            block_pe(NBLK - 3)
            block_pe(NBLK - 2, ahead=2 * TT - AHEAD)

            TURN_BANK = ((3, 4, 5, 6), (0, 1, 2, 4), (3, 5, 6, 7), (0, 1, 2, 4))

            def turn_y2(g):
                pe.wait_ge(sm["y2_ready"], g + 1)
                for k in range(KC):
                    for q in range(2):
                        for n in range(4):
                            mm = pe.transpose(ps[:, TURN_BANK[g][2 * k + q], n * P:(n + 1) * P],
                                              pay[g][:, 4 * q + n, k * P:(k + 1) * P], ident[:, :])
                        mm.then_inc(sm["tT_ready"], 1)

            def logits(g):
                pe.wait_ge(sm["tT_kept"], 4 * g + 4)
                for j in range(J):
                    for k in range(KC):
                        mm = pe.matmul(ps[:, TURN_BANK[g][0], j * E:(j + 1) * E], y2T[g][:, k, j * P:(j + 1) * P], wgs[:, k, :],
                                       start=(k == 0), stop=(k == 1))
                mm.then_inc(sm["lg_ready"], 1)

            def prefix(g):
                pe.wait_ge(sm["count_ready"], g + 1)
                bank = TURN_BANK[g][0]
                pe.matmul(ps[:, bank, 64:64 + E], upper[:, :], cnt[:, :], start=True, stop=True)
                pe.matmul(ps[:, bank, 80:80 + E], ones[:, :], cnt[:, :], start=True, stop=True).then_inc(sm["prefix_ready"], 1)

            def turn_we(experts):
                for e in experts:
                    if e >= 3:
                        pe.wait_ge(sm["weT_kept"], e - 2)
                    for k in range(KC):
                        for c in range(KC):
                            mm = pe.transpose(ps[:, 5 + e % 3, (k * KC + c) * P:(k * KC + c + 1) * P],
                                              we_load[:, e, c, k * P:(k + 1) * P], ident[:, :])
                    mm.then_inc(sm["weT_ready"], 1)

            def last_maxima():
                pe.wait_ge(sm["max_done"], 2 * LAST)
                turn_y2(0)

            block_pe(NBLK - 1, ahead=0, extra={2: last_maxima, 5: lambda: logits(0), 7: lambda: prefix(0)})
            pv(NBLK - 1, TT - 1)
            pe.wait_ge(sm["exp_done"], HG * TT * NBLK)
            turn_y2(1)
            logits(1)
            pe.wait_ge(sm["acc_ready"], NBLK)
            pe.wait_ge(sm["sidx_ready"], 1)
            turn_y2(2)
            prefix(1)
            logits(2)
            prefix(2)
            pe.wait_ge(sm["sidx_ready"], 2)
            turn_y2(3)
            logits(3)
            pe.wait_ge(sm["we_loaded"], 16)
            turn_we((0, 1))
            prefix(3)
            turn_we((2, 3, 4, 5, 6, 7))
            pe.wait_ge(sm["weT_kept"], E)
            pe.wait_ge(sm["sidx_ready"], NTG)

            with pe.Fori(0, E // 4) as u:
                for par in range(4):
                    e, half = 4 * u + par, par % 2
                    pe.wait_ge(sm[f"y_free{half}"], 2 * u + par // 2 + 1)
                    pe.wait_ge(sm[f"x_loaded{par}"], 32 * u + 32)
                    for k in range(KC):
                        for n in range(4):
                            mm = pe.transpose(ps[:, 2 * half + k, n * P:(n + 1) * P], x_load[par][:, n, k * P:(k + 1) * P],
                                              ident[:, :])
                        mm.then_inc(sm["xT_ready"], 1)
                    pe.wait_ge(sm["we_kept"], e + 1)
                    pe.wait_ge(sm["xT_kept"], 2 * e + 2)
                    for n in range(4):
                        o = ps[:, 4 + 2 * half + n // 2, (n % 2) * H:(n % 2 + 1) * H]
                        for k in range(KC):
                            mm = pe.matmul(o, xe_T[half][:, k, n * P:(n + 1) * P], we_now[:, half, k * H:(k + 1) * H],
                                           start=(k == 0), stop=(k == 1))
                        if n % 2:
                            mm.then_inc(sm[f"e_ready{half}"], 1)

        @block.scalar
        def _(act):
            def keep_turned(st):
                for m in range(4):
                    act.wait_ge(sm["chunk_ready"], CHUNK["t", st, m] + 1)
                    act.activation(yT_dst(st, m), ps_turned(st, m), ACT.Copy).then_inc(sm["chunk_kept"], 1)

            def yT_dst(st, m):
                k, q = m // 2, m % 2
                if st in (KEYS, VALUES):
                    return (vT if st else yT_v)[:, k, q * 512:(q + 1) * 512]
                return yT_v[:, k].rearrange("p (t j) -> p j t", j=J)[:, 4 * q:4 * q + 4]

            def ps_turned(st, m):
                src = ps[:, 6 + CHUNK["t", st, m] % 2, :]
                return src if st in (KEYS, VALUES) else src.rearrange("p (j t) -> p j t", j=4)

            def keep_projected(st, bias, chunks=range(4)):
                if st > 1 and chunks[0] == 0:
                    act.wait_ge(sm["split_done"], st - 1)
                    if st == 2:
                        act.wait_ge(sm["pieces_stored"], 48)
                    else:
                        act.wait_ge(sm[f"q_stored{st - 3}"], 12 * 16)
                for m in chunks:
                    c, half, chunk = m // 2, m % 2, CHUNK["p", st, m]
                    act.wait_ge(sm["chunk_ready"], chunk + 1)
                    src = ps[:, 6 + chunk % 2, :]
                    act.activation(q32[SLOT[st]][:, c, half * 512:(half + 1) * 512], src, ACT.Relu, bias=bias[:, c:c + 1])
                    act.activation(pieces[SLOT[st]][:, 0, c, half * 512:(half + 1) * 512], src, ACT.Relu, bias=bias[:, c:c + 1]
                                   ).then_inc(sm["chunk_kept"], 1)

            def keep_v(m):
                chunk = CHUNK["p", VALUES, m]
                act.wait_ge(sm["chunk_ready"], chunk + 1)
                for u in range(2):
                    dst = vaug[:, :, :].rearrange("p g (t j c) -> p g t j c", t=TT, j=HG)[:, :, 2 * m + u, :, 0:DH]
                    ins = act.activation(dst, ps[:, 6 + chunk % 2, u * H:(u + 1) * H].rearrange("p (g j c) -> p g j c", g=NG, j=HG),
                                         ACT.Relu)
                ins.then_inc(sm["chunk_kept"], 1)

            def keep_u(g):
                if g:
                    act.wait_ge(sm["emb_ready"], g)
                for q in range(2):
                    act.wait_ge(sm["uT_ready"], 2 * g + q + 1)
                    act.activation(uT[:, q * 512:(q + 1) * 512], ps[0:R, q, :], ACT.Identity, scale=srank[:, 0:1]
                                   ).then_inc(sm["uT_kept"], 1)

            def norm_rows(g):
                act.wait_ge(sm["prelude_rstd"], g + 1)
                act.wait_ge(sm["chunk_ready"], CHUNK["t", g, 3] + 1)
                for j in range(J):
                    ins = act.activation(y_v[:, j, :], ps[:, 2 + j // 2, (j % 2) * H:(j % 2 + 1) * H], ACT.Identity,
                                         bias=nmr[:, g % 2, j:j + 1], scale=rstd[:, g % 2, j:j + 1])
                ins.then_inc(sm["y_ready"], 1)

            act.wait_ge(sm["s_loaded"], 32)
            for g in range(NTG):
                keep_u(g)
                if g == 0:
                    act.wait_ge(sm["c_loaded"], 4 * 16)
                keep_turned(g)
                keep_projected(g, bq if g else bk, range(0, 2))
                norm_rows(g)
                keep_projected(g, bq if g else bk, range(2, 4))
                if g:
                    keep_v(g - 1)
                else:
                    keep_turned(VALUES)
                    act.wait_ge(sm["ones_set"], 1)
            keep_turned(NTG)
            keep_projected(NTG, bq)
            keep_v(NTG - 1)
            act.wait_ge(sm["split_done"], NTG + 1)

            def exps(i, t):
                for j in range(HG):
                    act.wait_ge(sm["scores_ready"], HG * (TT * i + t) + j + 1)
                    if not (isinstance(i, int) and i == 0 and t < RING) and j == 0:
                        act.wait_ge(sm["pv_done"], TT * i + t - RING + 1)
                    act.activation(probs[:, 2 * (t % RING) + j // 2, (j % 2) * SB:(j % 2 + 1) * SB],
                                   ps[:, EXP_BANK[j], :], ACT.Exp, scale=SCALE).then_inc(sm["exp_done"], 1)
                    if j == HG - 2 and t == 0 and isinstance(i, int) and i == NBLK - 1:
                        keep_acc(i - 1)

            def keep_acc(i):
                act.wait_ge(sm["pv_done"], TT * (i + 1))
                act.wait_ge(sm["acc_ready"], i)
                if not (isinstance(i, int) and i < 2):
                    act.wait_ge(sm["acc_stored"], 16 * (i - 1))
                act.activation(acc[:, ds(i % 2, 1)].rearrange("p o s -> p (o s)"), ps[:, PV_BANK, :], ACT.Copy
                               ).then_inc(sm["acc_ready"], 1)

            def shares(g):
                act.wait_ge(sm["lg_shifted"], g + 1)
                act.activation(ex[:, :, :], lg[:, :, :], ACT.Exp).then_inc(sm["ex_ready"], 1)

            def block_act(i, extra={}):
                for t in range(TT):
                    if t in extra:
                        extra[t]()
                    exps(i, t)

            block_act(0)
            block_act(1)
            with act.Fori(1, NBLK // 2 - 1) as u:
                for par in range(2):
                    block_act(2 * u + par)
            block_act(NBLK - 2)
            block_act(NBLK - 1, extra={6: lambda: shares(0)})
            keep_acc(NBLK - 1)

            def norm_act(g):
                act.wait_ge(sm["rstd_ready"], g + 1)
                for j in range(J):
                    ins = act.activation(pay[g][:, j, 0:H], pay[g][:, j, H:2 * H], ACT.Identity,
                                         bias=nmr[:, g % 2, j:j + 1], scale=rstd[:, g % 2, j:j + 1])
                ins.then_inc(sm["y2_ready"], 1)

            def keep_y2(g):
                act.wait_ge(sm["lg_ready"], g)
                for n in range(4):
                    act.wait_ge(sm["tT_ready"], 4 * g + n + 1)
                    act.activation(y2T[g][:, n // 2, (n % 2) * 512:(n % 2 + 1) * 512], ps[:, ((0, 1, 2, 4), (3, 5, 6, 7))[g == 2][n], :],
                                   ACT.Copy).then_inc(sm["tT_kept"], 1)

            def keep_we(experts):
                for e in experts:
                    act.wait_ge(sm["weT_ready"], e + 1)
                    act.activation(we_T[:, e], ps[:, 5 + e % 3], ACT.Copy).then_inc(sm["weT_kept"], 1)

            keep_y2(1)
            shares(1)
            keep_y2(2)
            shares(2)
            norm_act(3)
            keep_y2(3)
            shares(3)
            keep_we(range(E))
            with act.Fori(0, E // 4) as u:
                for par in range(4):
                    e, half = 4 * u + par, par % 2
                    act.wait_ge(sm[f"y_free{half}"], 2 * u + par // 2 + 1)
                    act.activation(we_now[:, half], we_T[:, ds(e, 1)].rearrange("p o n -> p (o n)"), ACT.Copy
                                   ).then_inc(sm["we_kept"], 1)
                    for k in range(KC):
                        act.wait_ge(sm["xT_ready"], 2 * e + k + 1)
                        act.activation(xe_T[half][:, k], ps[:, 2 * half + k], ACT.Copy).then_inc(sm["xT_kept"], 1)

        @block.vector
        def _(dve):
            dve.memset(ones[:, :], 1.0).then_inc(sm["ones_made"], 1)
            for w in range(3):
                dve.wait_ge(sm["wT_ready"], w + 1)
                dve.tensor_copy(wT[:, (1, 0, 2)[w]].rearrange("p c h -> p (c h)"), ps[:, w, :]).then_inc(sm["wT_kept"], 1)
            dve.memset(vaug[:, :, :], 1.0).then_inc(sm["ones_set"], 1)
            dve.memset(base[:, :], 0.0).then_inc(sm["ones_made"], 1)
            early_chain = Chain(dve, sm["prelude_chain"])

            def rsqrt_steps(link, rstd):
                link(dve.tensor_scalar(std[:, :], mv[:, :, 1], EPS, None, ALU.add))
                link(dve.tensor_scalar(ri[:, :], std[:, :].bitcast(I32), 1, None, ALU.arith_shift_right))
                link(dve.tensor_scalar(rstd.bitcast(I32), ri[:, :], -1.0, float(0x5f3759df), ALU.mult, ALU.add))
                for _ in range(3):
                    link(dve.tensor_tensor(rt[:, :], rstd, rstd, ALU.mult))
                    link(dve.tensor_tensor(rt[:, :], rt[:, :], std[:, :], ALU.mult))
                    link(dve.tensor_scalar(rt[:, :], rt[:, :], -0.5, 1.5, ALU.mult, ALU.add))
                    link(dve.tensor_tensor(rstd, rstd, rt[:, :], ALU.mult))

            def split(st):
                dve.wait_ge(sm["chunk_kept"], CHUNK["p", st, 3] + 1)
                v, pc = q32[SLOT[st]], pieces[SLOT[st]]
                early_chain.link(dve.tensor_tensor(v, v, pc[:, 0], ALU.subtract))
                early_chain.link(dve.tensor_copy(pc[:, 1], v))
                dve.tensor_tensor(pc[:, 2], v, pc[:, 1], ALU.subtract).then_inc(sm["split_done"], 1)

            def row_statistics(g):
                dve.wait_ge(sm["emb_ready"], g + 1)
                for j in range(J):
                    early_chain.mark(dve.bn_stats(stats[:, j, :], ps[:, 2 + j // 2, (j % 2) * H:(j % 2 + 1) * H]))
                dve.wait_ge(sm["prelude_chain"], early_chain.n)
                for j in range(J):
                    early_chain.mark(dve.bn_aggr(mv[:, j, :], stats[:, j, :]))
                dve.wait_ge(sm["prelude_chain"], early_chain.n)
                rsqrt_steps(early_chain.link, rstd[:, g % 2])
                dve.scalar_tensor_tensor(out=nmr[:, g % 2], in0=mv[:, :, 0], scalar=-1.0, in1=rstd[:, g % 2],
                                         op0=ALU.mult, op1=ALU.mult).then_inc(sm["prelude_rstd"], 1)
                dve.wait_ge(sm["prelude_rstd"], g + 1)

            def add_rows(g):
                dve.wait_ge(sm["y_ready"], g + 1)
                dve.tensor_tensor(res[g], ps[:, 2:6, :].rearrange("p b n -> p (b n)"), y_v.rearrange("p j h -> p (j h)"),
                                  ALU.add).then_inc(sm["res_made"], 1)

            row_statistics(0)
            dve.memset(zeros, 0.0).then_inc(sm["zeros_set"], 1)
            add_rows(0)
            for g in range(1, NTG):
                row_statistics(g)
                split(g - 1)
                add_rows(g)
            split(NTG - 1)
            split(NTG)

            def negate(m, u):
                mxm = mx[:, ds(m % 2, 1), :].rearrange("p o c -> p (o c)")
                if u == 0:
                    dve.wait_ge(sm["max_done"], 2 * TT * (m + 1))
                    dve.tensor_scalar(mpc[:, 0:16], mxm, -1.0, None, ALU.mult).then_inc(sm["max_chain"], 1)
                elif u == 1:
                    dve.wait_ge(sm["max_chain"], m + 1)
                    dve.scalar_tensor_tensor(out=mpc[:, 16:32], in0=mxm, scalar=-1.0, in1=mpc[:, 0:16],
                                             op0=ALU.mult, op1=ALU.subtract).then_inc(sm["mpc_ready"], 1)
                elif u == 2:
                    dve.wait_ge(sm["mpc_ready"], m + 1)
                    if not (isinstance(m, int) and m == 0):
                        dve.wait_ge(sm["m_loaded"], 128 * m)
                    dve.transpose(mrow[:, :], mpc[:, :]).then_inc(sm["mrow_ready"], 1)

            KEEP_T, KEEP_BACK = AHEAD % TT, AHEAD // TT + 1

            def keep_acc_dve(i):
                dve.wait_ge(sm["pv_done"], TT * (i + 1))
                if not (isinstance(i, int) and i < 2):
                    dve.wait_ge(sm["acc_stored"], 16 * (i - 1))
                dve.tensor_copy(acc[:, ds(i % 2, 1)].rearrange("p o s -> p (o s)"), ps[:, PV_BANK, :]
                                ).then_inc(sm["acc_ready"], 1)

            def block_dve(m, first=False, after=None):
                for t in range(TT):
                    for u in range(2):
                        col = 4 * (2 * (t % 2) + u) + t // 2
                        dve.wait_ge(sm["max_ready"], 2 * (TT * m + t) + u + 1)
                        dve.tensor_reduce(mx[:, ds(m % 2, 1), col:col + 1].rearrange("p o c -> p (o c)"),
                                          ps[:, MAX_BANK + 2 * u:MAX_BANK + 2 * u + 2, :].rearrange("p b n -> p (b n)"),
                                          AX.X, ALU.max).then_inc(sm["max_done"], 1)
                        if 2 * t + u < 3 and not first:
                            negate(m - 1, 2 * t + u)
                        if t == KEEP_T and u == 0 and not (isinstance(m, int) and m < KEEP_BACK):
                            keep_acc_dve(m - KEEP_BACK)
                    if after:
                        after(t)

            block_dve(0, first=True)
            for m in range(1, 4):
                block_dve(m)
            with dve.Fori(2, NBLK // 2 - 1) as u2:
                for par in range(2):
                    block_dve(2 * u2 + par)

            def invert0(t):
                if t == 1:
                    dve.wait_ge(sm["den_loaded"], 16)
                if 1 <= t <= 4:
                    dve.reciprocal(rden[0:96, (t - 1) * P:t * P], rden[0:96, (t - 1) * P:t * P]).then_inc(sm["tail_chain"], 1)
                if t == 5:
                    dve.wait_ge(sm["tail_chain"], 4)
                    dve.sem_inc(sm["rden_ready"], 1)

            block_dve(NBLK - 2, after=invert0)
            block_dve(NBLK - 1)
            for u in range(3):
                negate(NBLK - 1, u)

            tail_count = [4]

            def mark(ins):
                tail_count[0] += 1
                ins.then_inc(sm["tail_chain"], 1)

            def settle():
                dve.wait_ge(sm["tail_chain"], tail_count[0])

            def link(ins):
                mark(ins)
                settle()

            def residual(g):
                dve.wait_ge(sm[f"att_loaded{g}"], 16 * 16)
                dve.tensor_tensor(num[g % 2], num[g % 2], rdb[g % 2], ALU.mult).then_inc(sm["num_scaled"], 1)
                dve.wait_ge(sm["num_scaled"], g + 1)
                dve.tensor_tensor(pay[g][:, :, H:2 * H], res[g].rearrange("p (j h) -> p j h", j=J),
                                  num[g % 2].rearrange("p (j h) -> p j h", j=J), ALU.add).then_inc(sm["h2_ready"], 1)

            def statistics(g):
                hj = pay[g][:, :, H:2 * H]
                dve.wait_ge(sm["h2_ready"], g + 1)
                for j in range(J):
                    mark(dve.bn_stats(stats[:, j, :], hj[:, j]))
                settle()
                for j in range(J):
                    mark(dve.bn_aggr(mv[:, j, :], stats[:, j, :]))
                settle()
                rsqrt_steps(link, rstd[:, g % 2])

            def norm_dve(g):
                for j in range(J):
                    mark(dve.tensor_scalar(pay[g][:, j, 0:H], pay[g][:, j, H:2 * H], mv[:, j, 0:1], rstd[:, g % 2, j:j + 1],
                                           ALU.subtract, ALU.mult))
                settle()
                dve.sem_inc(sm["y2_ready"], 1)
                dve.sem_inc(sm["rstd_ready"], 1)

            def rstd_for_act(g):
                dve.scalar_tensor_tensor(out=nmr[:, g % 2], in0=mv[:, :, 0], scalar=-1.0, in1=rstd[:, g % 2],
                                         op0=ALU.mult, op1=ALU.mult).then_inc(sm["rstd_ready"], 1)
                dve.wait_ge(sm["rstd_ready"], g + 1)

            TURN_BANK = ((3, 4, 5, 6), (0, 1, 2, 4), (3, 5, 6, 7), (0, 1, 2, 4))

            def keep_y2_dve(g):
                dve.wait_ge(sm["h2_ready"], 2)
                for n in range(4):
                    dve.wait_ge(sm["tT_ready"], 4 * g + n + 1)
                    dve.tensor_copy(y2T[g][:, n // 2, (n % 2) * 512:(n % 2 + 1) * 512], ps[:, TURN_BANK[g][n], :]
                                    ).then_inc(sm["tT_kept"], 1)

            bj = lambda a: a[:, :].unsqueeze(2).broadcast_to([P, J, E])
            be_ = lambda a: a[:, :].unsqueeze(1).broadcast_to([P, J, E])

            def shift_logits(g):
                bank = TURN_BANK[g][0]
                dve.wait_ge(sm["lg_ready"], g + 1)
                lps = ps[:, bank, 0:J * E].rearrange("p (j e) -> p j e", j=J)
                link(dve.tensor_reduce(c1[:, :], lps, AX.X, ALU.max))
                dve.tensor_tensor(lg[:, :, :], lps, bj(c1), ALU.subtract).then_inc(sm["lg_shifted"], 1)

            def route(g):
                bank = TURN_BANK[g][0]
                dve.wait_ge(sm["ex_ready"], g + 1)
                link(dve.tensor_reduce(c2[:, :], ex[:, :, :], AX.X, ALU.add))
                link(dve.reciprocal(c3[:, :], c2[:, :]))
                link(dve.tensor_tensor(ex[:, :, :], ex[:, :, :], bj(c3), ALU.mult))
                link(dve.tensor_reduce(c1[:, :], ex[:, :, :], AX.X, ALU.max))
                link(dve.tensor_tensor(oh[:, :, :], ex[:, :, :], bj(c1), ALU.is_ge))
                link(dve.tensor_tensor(oh[:, :, :], oh[:, :, :], be_(rank8), ALU.mult))
                link(dve.tensor_reduce(c2[:, :], oh[:, :, :], AX.X, ALU.max))
                link(dve.tensor_tensor(oh[:, :, :], oh[:, :, :], bj(c2), ALU.is_equal))
                dve.tensor_reduce(cnt[:, :], oh[:, :, :].rearrange("p j e -> p e j"), AX.X, ALU.add).then_inc(sm["count_ready"], 1)
                link(dve.tensor_tensor(tmp[:, :, :], oh[:, :, :], be_(eid), ALU.mult))
                link(dve.tensor_reduce(c3[:, :], tmp[:, :, :], AX.X, ALU.add))
                dve.wait_ge(sm["prefix_ready"], g + 1)
                link(dve.tensor_tensor(loc[:, 0, :], ps[:, bank, 64:64 + E], base[:, :], ALU.add))
                for j in range(1, J):
                    link(dve.tensor_tensor(loc[:, j, :], loc[:, j - 1, :], oh[:, j - 1, :], ALU.add))
                link(dve.tensor_tensor(base[:, :], ps[:, bank, 80:80 + E], base[:, :], ALU.add))
                link(dve.tensor_tensor(loc[:, :, :], loc[:, :, :], oh[:, :, :], ALU.mult))
                link(dve.tensor_reduce(c2[:, :], loc[:, :, :], AX.X, ALU.add))
                link(dve.tensor_scalar(kept[:, :], c2[:, :], float(CAP), None, ALU.is_lt))
                mark(dve.tensor_tensor(pay[g][:, :, 2 * H], c1[:, :], kept[:, :], ALU.mult))
                mark(dve.tensor_copy(pay[g][:, :, 2 * H + 1], tid[:, :]))
                link(dve.scalar_tensor_tensor(out=slot[:, :], in0=c3[:, :], scalar=float(CAP), in1=c2[:, :],
                                              op0=ALU.mult, op1=ALU.add))
                link(dve.tensor_scalar(c2[:, :], kept[:, :], float(-2 * E * CAP), float(2 * E * CAP), ALU.mult, ALU.add))
                dve.tensor_tensor(sidx[:, g], slot[:, :], c2[:, :], ALU.add).then_inc(sm["sidx_ready"], 1)
                link(dve.tensor_scalar(tid[:, :], tid[:, :], float(TG), None, ALU.add))

            statistics(0)
            norm_dve(0)
            keep_y2_dve(0)
            statistics(1)
            shift_logits(0)
            norm_dve(1)
            route(0)
            statistics(2)
            norm_dve(2)
            dve.wait_ge(sm["den_loaded"], 48)
            dve.reciprocal(rden[96:P], rden[96:P]).then_inc(sm["rden_ready"], 1)
            shift_logits(1)
            route(1)
            residual(3)
            statistics(3)
            rstd_for_act(3)
            shift_logits(2)
            route(2)
            shift_logits(3)
            route(3)

            dve.wait_ge(sm["scattered"], 16 * NTG * J)
            dve.sem_inc(sm["y_free0"], 1)
            dve.sem_inc(sm["y_free1"], 1)
            with dve.Fori(0, E // 4) as u:
                for par in range(4):
                    e, half = 4 * u + par, par % 2
                    dve.wait_ge(sm[f"x_loaded{par}"], 32 * u + 32)
                    tok = x_load[par][:, :, 2 * H + 1]
                    dve.tensor_scalar(empty[:, par], tok, 0.0, float(2 * B * S), ALU.is_equal, ALU.mult).then_inc(sm["e_chain"], 1)
                    dve.wait_ge(sm["e_chain"], 4 * e + 1)
                    dve.scalar_tensor_tensor(out=oidx[:, par], in0=tok, scalar=-1.0, in1=empty[:, par],
                                             op0=ALU.add, op1=ALU.add).then_inc(sm["e_chain"], 1)
                    for n in range(2):
                        dve.wait_ge(sm[f"e_ready{half}"], 2 * (2 * u + par // 2) + n + 1)
                        dve.tensor_tensor(y_sum[:, half, 2 * n:2 * n + 2],
                                          ps[:, 4 + 2 * half + n].rearrange("p (n h) -> p n h", n=2),
                                          bb[:, par].unsqueeze(1).broadcast_to([P, 2, H]), ALU.add).then_inc(sm["e_chain"], 1)
                    dve.wait_ge(sm["e_chain"], 4 * e + 4)
                    dve.sem_inc(sm[f"y_free{half}"], 1)
                    for n in range(4):
                        dve.scalar_tensor_tensor(out=y_out[:, par, n], in0=y_sum[:, half, n],
                                                 scalar=x_load[par][:, n, 2 * H:2 * H + 1],
                                                 in1=x_load[par][:, n, H:2 * H], op0=ALU.mult, op1=ALU.add
                                                 ).then_inc(sm["y_chain"], 1)
                    dve.wait_ge(sm["y_chain"], 4 * e + 4)
                    dve.sem_inc(sm["y_out_ready"], 1)


_INS = ['x', 'L0_tok_U', 'L0_tok_s', 'L0_tok_Vt', 'L0_attn_keys', 'L0_attn_values', 'L0_attn_Wq_w', 'L0_attn_Wq_b',
        'L0_attn_Wk_w', 'L0_attn_Wk_b', 'L0_attn_Wv_w', 'L0_attn_Wv_b', 'L0_ffn_wg', 'L0_ffn_W', 'L0_ffn_b']


def kernel(**inputs):
    import numpy as _np
    import concourse.bacc as _bacc
    from concourse import mybir as _mybir
    from concourse.bass_utils import run_bass_kernel_spmd as _run

    nc = _bacc.Bacc("TRN2", target_bir_lowering=False, num_devices=1)
    arrays, args = {}, []
    for name in _INS:
        a = _np.ascontiguousarray(inputs[name])
        arrays[f"in_{name}"] = a
        args.append(nc.dram_tensor(f"in_{name}", a.shape, _mybir.dt.from_np(a.dtype), kind="ExternalInput").ap())
    args.append(nc.dram_tensor("out_h", (B * S, H), _mybir.dt.float32, kind="ExternalOutput").ap())
    build(nc, *args)
    r = _run(nc, [arrays], core_ids=[0])
    return r.results[0]["out_h"].reshape(B, S, H)
```
